# Optimizing a Trainium2 kernel written in Bass

```python
import numpy as np
import jax
import jax.numpy as jnp

def _softmax(x, axis=-1):
    return jax.nn.softmax(x, axis=axis)

def _gelu(x):
    return jax.nn.gelu(x, approximate=True)

def _silu(x):
    return jax.nn.silu(x)

def _sigmoid(x):
    return jax.nn.sigmoid(x)

def _layernorm(x, axis=-1, eps=1e-05):
    m = jnp.mean(x, axis=axis, keepdims=True)
    v = jnp.var(x, axis=axis, keepdims=True)
    return (x - m) / jnp.sqrt(v + eps)

def _scatter_add(tgt, idx, src, axis=0):
    return tgt.at[idx].add(src)

def _segment_sum(src, seg, n):
    return jax.ops.segment_sum(src, seg, n)
kernel_name = 'mk_decoder_postln_d1_seqx_r4_b85021'

def setup_inputs(seed: int=0):
    np.random.seed(seed)
    _w = jnp.asarray

    def _rec_inputs():
        import jax
        import jax.numpy as jnp
        _rk = jax.random.key(seed)
        x = 7.22e-05 + 1 * jax.random.normal(jax.random.fold_in(_rk, 1), (16, 112, 256), jnp.float32)
        _lenS = 112 - jax.random.randint(jax.random.fold_in(_rk, 7), (16,), 0, max(1, 112 // 4) + 1, jnp.int32)
        _lenS2 = 375 - jax.random.randint(jax.random.fold_in(_rk, 8), (16,), 0, max(1, 375 // 4) + 1, jnp.int32)
        _ctx_1024P = jax.random.normal(jax.random.fold_in(_rk, 11), (16, 16, 256), jnp.float32)
        _ctx_1024c = jax.random.dirichlet(jax.random.fold_in(_rk, 511), 0.3 * jnp.ones((16,), jnp.float32), (16, 375))
        _ctx_1024t = jnp.einsum('bsk,bkd->bsd', _ctx_1024c, _ctx_1024P)
        _ctx_1024t = _ctx_1024t * jax.lax.rsqrt(jnp.mean(jnp.square(_ctx_1024t)) + 1e-12) * 0.953939
        ctx_1024 = 4.13588e-05 + 0.999923 * (_ctx_1024t + 0.3 * jax.random.normal(jax.random.fold_in(_rk, 611), (16, 375, 256), jnp.float32))
        return (x, ctx_1024)
    x, ctx_1024 = _rec_inputs()

    def _L0_attn_setup():
        import jax, jax.numpy as jnp
        import numpy as np

        def soft_clamp(x, lo, hi, sharpness):
            c = (hi + lo) / 2.0
            r = (hi - lo) / 2.0
            xn = (x - c) / (r + 1e-08)
            return jnp.tanh(xn * sharpness) / sharpness * r + c
        key = jax.random.key(seed)
        ks = jax.random.split(key, 7)
        B, L, D, N = (2, 512, 256, 16)
        x = jax.random.normal(ks[0], (B, L, D), dtype=jnp.float32)
        Wdt = jax.random.normal(ks[1], (D, D), dtype=jnp.float32) * 0.02
        bdt = jnp.full((D,), -2.0, dtype=jnp.float32)
        WB = jax.random.normal(ks[2], (N, D), dtype=jnp.float32) * (1.0 / np.sqrt(D))
        WC = jax.random.normal(ks[3], (N, D), dtype=jnp.float32) * (1.0 / np.sqrt(D))
        A_log = jax.random.normal(ks[4], (D, N), dtype=jnp.float32) * 0.1
        Dp = jnp.full((D,), 0.1, dtype=jnp.float32)
        return {'x': x, 'Wdt': Wdt, 'bdt': bdt, 'WB': WB, 'WC': WC, 'A_log': A_log, 'Dp': Dp}
    _L0_attn_all = _L0_attn_setup()
    _L0_attn_in = {k: v for k, v in _L0_attn_all.items() if k in ('Wdt', 'bdt', 'WB', 'WC', 'A_log', 'Dp')}
    del _L0_attn_all

    def _L0_xattn_setup():
        import jax, jax.numpy as jnp
        import numpy as np
        B, S, D, DFF = (4, 512, 256, 1024)
        EPS = 1e-05

        def layernorm(x, gamma, beta):
            mu = jnp.mean(x, axis=-1, keepdims=True)
            var = jnp.var(x, axis=-1, keepdims=True)
            return (x - mu) * jax.lax.rsqrt(var + EPS) * gamma + beta

        def attention(Q, K, V, causal):
            d_k = Q.shape[-1]
            scores = jnp.einsum('bqd,bkd->bqk', Q, K) / jnp.sqrt(jnp.asarray(d_k, Q.dtype))
            if causal:
                q_len, k_len = (scores.shape[-2], scores.shape[-1])
                mask = jnp.tril(jnp.ones((q_len, k_len), dtype=bool))
                scores = jnp.where(mask[None], scores, jnp.asarray(-jnp.inf, scores.dtype))
            w = jax.nn.softmax(scores, axis=-1)
            return jnp.einsum('bqk,bkd->bqd', w, V)
        key = jax.random.key(seed)
        ks = jax.random.split(key, 12)
        sd = 0.02
        return {'y': jax.random.normal(ks[0], (B, S, D), jnp.float32), 'Z': jax.random.normal(ks[1], (B, S, D), jnp.float32), 'w1': jax.random.normal(ks[2], (D, DFF), jnp.float32) * sd, 'b1': jnp.zeros((DFF,), jnp.float32), 'w2': jax.random.normal(ks[3], (DFF, D), jnp.float32) * sd, 'b2': jnp.zeros((D,), jnp.float32), 'g1': jnp.ones((D,), jnp.float32), 'beta1': jnp.zeros((D,), jnp.float32), 'g2': jnp.ones((D,), jnp.float32), 'beta2': jnp.zeros((D,), jnp.float32), 'g3': jnp.ones((D,), jnp.float32), 'beta3': jnp.zeros((D,), jnp.float32)}
    _L0_xattn_all = _L0_xattn_setup()
    _L0_xattn_in = {k: v for k, v in _L0_xattn_all.items() if k in ('w1', 'b1', 'w2', 'b2', 'g1', 'beta1', 'g2', 'beta2', 'g3', 'beta3')}
    del _L0_xattn_all

    def _L0_ffn_setup():
        import jax, jax.numpy as jnp
        import numpy as np
        from jax import lax
        T, B, I, M, O = (64, 64, 256, 256, 256)

        def _xavier(key, shape):
            fan_out, fan_in = shape
            limit = float(np.sqrt(6.0 / (fan_in + fan_out)))
            return jax.random.uniform(key, shape, jnp.float32, -limit, limit)
        key = jax.random.key(seed)
        ks = jax.random.split(key, 9)
        x = jax.random.normal(ks[0], (T, B, I), jnp.float32)
        return {'x': x, 'wf': _xavier(ks[1], (M, I)), 'uf': _xavier(ks[2], (M, M)), 'bf': jnp.zeros((M,), jnp.float32), 'wi': _xavier(ks[3], (M, I)), 'ui': _xavier(ks[4], (M, M)), 'bi': jnp.zeros((M,), jnp.float32), 'wc': _xavier(ks[5], (M, I)), 'uc': _xavier(ks[6], (M, M)), 'bc': jnp.zeros((M,), jnp.float32), 'wo': _xavier(ks[7], (O, I)), 'uo': _xavier(ks[8], (O, M)), 'bo': jnp.zeros((O,), jnp.float32), 'in_c': jnp.zeros((M,), jnp.float32)}
    _L0_ffn_all = _L0_ffn_setup()
    _L0_ffn_in = {k: v for k, v in _L0_ffn_all.items() if k in ('wf', 'uf', 'bf', 'wi', 'ui', 'bi', 'wc', 'uc', 'bc', 'wo', 'uo', 'bo', 'in_c')}
    del _L0_ffn_all
    return {'x': x, 'ctx_1024': ctx_1024, 'L0_attn_Wdt': _L0_attn_in['Wdt'], 'L0_attn_bdt': _L0_attn_in['bdt'], 'L0_attn_WB': _L0_attn_in['WB'], 'L0_attn_WC': _L0_attn_in['WC'], 'L0_attn_A_log': _L0_attn_in['A_log'], 'L0_attn_Dp': _L0_attn_in['Dp'], 'L0_xattn_w1': _L0_xattn_in['w1'], 'L0_xattn_b1': _L0_xattn_in['b1'], 'L0_xattn_w2': _L0_xattn_in['w2'], 'L0_xattn_b2': _L0_xattn_in['b2'], 'L0_xattn_g1': _L0_xattn_in['g1'], 'L0_xattn_beta1': _L0_xattn_in['beta1'], 'L0_xattn_g2': _L0_xattn_in['g2'], 'L0_xattn_beta2': _L0_xattn_in['beta2'], 'L0_xattn_g3': _L0_xattn_in['g3'], 'L0_xattn_beta3': _L0_xattn_in['beta3'], 'L0_ffn_wf': _L0_ffn_in['wf'], 'L0_ffn_uf': _L0_ffn_in['uf'], 'L0_ffn_bf': _L0_ffn_in['bf'], 'L0_ffn_wi': _L0_ffn_in['wi'], 'L0_ffn_ui': _L0_ffn_in['ui'], 'L0_ffn_bi': _L0_ffn_in['bi'], 'L0_ffn_wc': _L0_ffn_in['wc'], 'L0_ffn_uc': _L0_ffn_in['uc'], 'L0_ffn_bc': _L0_ffn_in['bc'], 'L0_ffn_wo': _L0_ffn_in['wo'], 'L0_ffn_uo': _L0_ffn_in['uo'], 'L0_ffn_bo': _L0_ffn_in['bo'], 'L0_ffn_in_c': _L0_ffn_in['in_c']}

def reference(x, ctx_1024, L0_attn_Wdt, L0_attn_bdt, L0_attn_WB, L0_attn_WC, L0_attn_A_log, L0_attn_Dp, L0_xattn_w1, L0_xattn_b1, L0_xattn_w2, L0_xattn_b2, L0_xattn_g1, L0_xattn_beta1, L0_xattn_g2, L0_xattn_beta2, L0_xattn_g3, L0_xattn_beta3, L0_ffn_wf, L0_ffn_uf, L0_ffn_bf, L0_ffn_wi, L0_ffn_ui, L0_ffn_bi, L0_ffn_wc, L0_ffn_uc, L0_ffn_bc, L0_ffn_wo, L0_ffn_uo, L0_ffn_bo, L0_ffn_in_c):
    import jax
    import jax.numpy as jnp

    def _L0_attn_ref(x, Wdt, bdt, WB, WC, A_log, Dp):
        import jax, jax.numpy as jnp
        import numpy as np

        def soft_clamp(x, lo, hi, sharpness):
            c = (hi + lo) / 2.0
            r = (hi - lo) / 2.0
            xn = (x - c) / (r + 1e-08)
            return jnp.tanh(xn * sharpness) / sharpness * r + c
        dt = soft_clamp(jax.nn.softplus(x @ Wdt.T + bdt), 0.001, 0.1, 0.5)
        B_param = x @ WB.T
        C_param = x @ WC.T
        A = -jnp.exp(soft_clamp(A_log, -5.0, 5.0, 0.5))
        dt_A = soft_clamp(dt[..., None] * A[None, None], -8.0, 8.0, 0.5)
        dA = jnp.exp(dt_A)
        dB = dt[..., None] * B_param[:, :, None, :]
        dA_t = jnp.moveaxis(dA, 1, 0)
        dB_t = jnp.moveaxis(dB, 1, 0)
        x_t = jnp.moveaxis(x, 1, 0)
        C_t = jnp.moveaxis(C_param, 1, 0)
        h0 = jnp.zeros(x.shape[:1] + (x.shape[2], A.shape[1]), dtype=jnp.float32)

        def step(h, inp):
            dAt, dBt, xt, Ct = inp
            h = dAt * h + dBt * xt[..., None]
            h_norm = jnp.sqrt(jnp.sum(h * h, axis=(1, 2), keepdims=True))
            scale = jnp.minimum(20.0 / (h_norm + 1e-08), 1.0)
            h = h * scale
            y = jnp.einsum('bdn,bn->bd', h, Ct) + Dp * xt
            return (h, y)
        _, ys = jax.lax.scan(step, h0, (dA_t, dB_t, x_t, C_t))
        return jnp.moveaxis(ys, 0, 1)

    def _L0_xattn_ref(y, Z, w1, b1, w2, b2, g1, beta1, g2, beta2, g3, beta3):
        import jax, jax.numpy as jnp
        import numpy as np
        B, S, D, DFF = (4, 512, 256, 1024)
        EPS = 1e-05

        def layernorm(x, gamma, beta):
            mu = jnp.mean(x, axis=-1, keepdims=True)
            var = jnp.var(x, axis=-1, keepdims=True)
            return (x - mu) * jax.lax.rsqrt(var + EPS) * gamma + beta

        def attention(Q, K, V, causal):
            d_k = Q.shape[-1]
            scores = jnp.einsum('bqd,bkd->bqk', Q, K) / jnp.sqrt(jnp.asarray(d_k, Q.dtype))
            if causal:
                q_len, k_len = (scores.shape[-2], scores.shape[-1])
                mask = jnp.tril(jnp.ones((q_len, k_len), dtype=bool))
                scores = jnp.where(mask[None], scores, jnp.asarray(-jnp.inf, scores.dtype))
            w = jax.nn.softmax(scores, axis=-1)
            return jnp.einsum('bqk,bkd->bqd', w, V)
        sa = attention(y, y, y, causal=True)
        y = layernorm(y + sa, g1, beta1)
        ca = attention(y, Z, Z, causal=False)
        y = layernorm(y + ca, g2, beta2)
        h = jax.nn.relu(jnp.einsum('bsd,df->bsf', y, w1) + b1)
        ff = jnp.einsum('bsf,fd->bsd', h, w2) + b2
        y = layernorm(y + ff, g3, beta3)
        return y

    def _L0_ffn_ref(x, wf, uf, bf, wi, ui, bi, wc, uc, bc, wo, uo, bo, in_c):
        import jax, jax.numpy as jnp
        import numpy as np
        from jax import lax
        T, B, I, M, O = (64, 64, 256, 256, 256)

        def _xavier(key, shape):
            fan_out, fan_in = shape
            limit = float(np.sqrt(6.0 / (fan_in + fan_out)))
            return jax.random.uniform(key, shape, jnp.float32, -limit, limit)
        batch = x.shape[1]
        c0 = jnp.broadcast_to(in_c, (batch, in_c.shape[0]))

        def step(c, xt):
            ft = jax.nn.sigmoid(xt @ wf.T + c @ uf.T + bf)
            it = jax.nn.sigmoid(xt @ wi.T + c @ ui.T + bi)
            gt = jnp.tanh(xt @ wc.T + c @ uc.T + bc)
            c = ft * c + it * gt
            return (c, None)
        c_final, _ = lax.scan(step, c0, x)
        h = jnp.tanh(jnp.einsum('tbi,oi->tbo', x, wo) + c_final @ uo.T + bo)
        return h
    x = _layernorm(x + _L0_attn_ref(x, L0_attn_Wdt, L0_attn_bdt, L0_attn_WB, L0_attn_WC, L0_attn_A_log, L0_attn_Dp), axis=-1)
    x = _layernorm(x + _L0_xattn_ref(x, ctx_1024, L0_xattn_w1, L0_xattn_b1, L0_xattn_w2, L0_xattn_b2, L0_xattn_g1, L0_xattn_beta1, L0_xattn_g2, L0_xattn_beta2, L0_xattn_g3, L0_xattn_beta3), axis=-1)
    x = _layernorm(x + _L0_ffn_ref(x, L0_ffn_wf, L0_ffn_uf, L0_ffn_bf, L0_ffn_wi, L0_ffn_ui, L0_ffn_bi, L0_ffn_wc, L0_ffn_uc, L0_ffn_bc, L0_ffn_wo, L0_ffn_uo, L0_ffn_bo, L0_ffn_in_c), axis=-1)
    return x

_drawn_inputs = setup_inputs


def setup_inputs(seed=0):
    import zlib

    import numpy as np

    out = dict(_drawn_inputs(seed))
    spreads = {'L0_attn_bdt': (-2.0, 0.2),
     'L0_attn_Dp': (0.10000000149011612, 0.6),
     'L0_xattn_b1': (0.0, 0.331),
     'L0_xattn_b2': (0.0, 0.1),
     'L0_xattn_g1': (1.0, 0.2),
     'L0_xattn_beta1': (0.0, 0.1),
     'L0_xattn_g2': (1.0, 0.2),
     'L0_xattn_beta2': (0.0, 0.1),
     'L0_xattn_g3': (1.0, 0.2),
     'L0_xattn_beta3': (0.0, 0.1),
     'L0_ffn_bf': (0.0, 0.716),
     'L0_ffn_bi': (0.0, 0.679),
     'L0_ffn_bc': (0.0, 0.1),
     'L0_ffn_bo': (0.0, 0.1),
     'L0_ffn_in_c': (0.0, 0.8)}
    factors = {}
    for name, (base, spread) in spreads.items():
        noise = np.random.default_rng([zlib.crc32(name.encode()), seed]).standard_normal(out[name].shape)
        drawn = base * np.exp(spread * noise) if base else spread * noise
        out[name] = jnp.asarray(drawn.astype(out[name].dtype))
    for name, factor in factors.items():
        out[name] = (out[name] * factor).astype(out[name].dtype)
    return out
```

```python
from contextlib import ExitStack

import numpy as np

import concourse.bass as bass
from concourse import mybir

F32 = mybir.dt.float32
BF16 = mybir.dt.bfloat16
ALU = mybir.AluOpType
ACT = mybir.ActivationFunctionType
P = 128

B, L, D, N = 16, 112, 256, 16
TOK = B * L
TILES = TOK // P
DH = D // P
CH = 2
CB = B // CH
TB = 16
BLOCKS = L // TB
AHEAD = 8
EPS = 1e-5
CLAMP = 20.0
DT_C, DT_R = (0.1 + 0.001) / 2.0, (0.1 - 0.001) / 2.0
B_PIECE = [0, 0, 0, 1, 1, 1, 2, 2]
V_PIECE = [0, 1, 2, 0, 1, 2, 0, 1]
COMBOS = len(B_PIECE)


def shape_constants():
    p = np.arange(P)
    ident = np.eye(P, dtype=np.float32)
    block_ones = (p[:, None] // N == p[None, :] // N).astype(np.float32)
    own_batch = (p[:, None] // N == np.arange(CB)[None, :]).astype(np.float32)
    row_batch = (p[:, None] % B == np.arange(B)[None, :]).astype(np.float32)
    causal = np.where(p[:, None] >= np.arange(L)[None, :], 0.0, -1e30).astype(np.float32)
    return np.ascontiguousarray(np.concatenate([ident, block_ones, own_batch, row_batch, causal], axis=1))


def state_space(nc, used, a, x1):
    with ExitStack() as ctx:
        def sb(name, shape, dt=F32):
            return ctx.enter_context(nc.sbuf_tensor(name, shape, dt))

        def pb(name, shape, dt=F32):
            return ctx.enter_context(nc.psum_tensor(name, shape, dt))

        def sem(name):
            used.append(nc.alloc_semaphore(name))
            return used[-1]

        v_scratch = nc.dram_tensor("v_pieces", (3, TOK, D), BF16, kind="Internal").ap()
        b_scratch = nc.dram_tensor("b_pieces", (3, TOK, N), BF16, kind="Internal").ap()
        c_scratch = nc.dram_tensor("c_param", (N, TOK), F32, kind="Internal").ap()

        const = sb("const", [P, a["consts"].shape[1]])
        ident = const[:, 0:P]
        block_ones = const[:, P:2 * P]
        own_batch = const[:, 2 * P:2 * P + CB]
        row_batch = const[:, 2 * P + CB:2 * P + CB + B]
        turned_c = sb("turned_c", [P, CH * TB * (P + CB)])
        x_rows = turned_c[:, 0:TILES * D]
        x_cols = sb("x_cols", [P, DH * TOK])
        v_hi = x_cols[:, 0:TILES * D // 2].bitcast(BF16)
        v_mid = x_cols[:, TILES * D // 2:TILES * D].bitcast(BF16)
        v_lo = x_rows[:, 0:TILES * D // 2].bitcast(BF16)
        proj_w = sb("proj_w", [P, DH, D + 2 * N])
        a_exp = sb("a_exp", [P, DH, N])
        bdt = sb("bdt", [P, D])
        dp1 = sb("dp1", [P, D])
        tanh_bias = sb("tanh_bias", [P, 1])
        dt_cols = sb("dt_cols", [P, DH, TOK + AHEAD])
        c_col = sb("c_col", [P, CH, L])
        b_rows = sb("b_rows", [P, L * N], BF16)
        v_rows = sb("v_rows", [P, (L + 1) * D], BF16)
        c_rows = v_rows[0:N, 0:2 * TOK].bitcast(F32)
        b_wide = [sb(f"b_wide{c}", [P, (L + 1) * P], BF16) for c in range(CH)]
        bn = TILES * N
        bc = b_wide[1][:, 0:2 * bn].bitcast(F32)
        b_work = b_wide[1][:, 2 * bn:4 * bn].bitcast(F32)
        b_pc = b_wide[1][:, 4 * bn:7 * bn].rearrange("p (q n) -> p q n", q=3)
        ring = sb("ring", [P, TB, DH, CH, CB * N])
        flat = ring[:, :, :, :, :].rearrange("p t h c n -> p (t h c n)")
        dt_rows = flat[:, 0:TILES * D]
        v_work = flat[:, TILES * D:2 * TILES * D]
        rows = [x_cols[:, i * D:(i + 1) * D] for i in range(DH * TOK // D)]
        turned_set = [turned_c[:, c * TB * (P + CB):(c + 1) * TB * (P + CB)] for c in range(CH)]
        turned_diagonal = [t.rearrange("p (t m) -> p t m", m=P + CB)[:, :, 0:CB] for t in turned_set]
        h = [rows[2 * c:2 * c + 2] for c in range(CH)]
        squares, x_blk, x_skip, res, normed = (rows[i:i + 2] for i in range(4, 14, 2))
        decayed = [sb(f"decayed{c}", [P, D]) for c in range(CH)]
        sumsq = [sb(f"sumsq{c}", [P, 1]) for c in range(CH)]
        clamped = [sb(f"clamped{c}", [P, 1]) for c in range(CH)]
        scale = [sb(f"scale{c}", [P, TB]) for c in range(CH)]
        own_scale = [sb(f"own_scale{c}", [P, TB, CB]) for c in range(CH)]
        row_scale = [sb(f"row_scale{c}", [P, 1]) for c in range(CH)]
        sixteenth = sb("sixteenth", [P, 1])
        minus_half = sb("minus_half", [P, 1])
        y_rows = [sb(f"y_rows{c}", [P, D]) for c in range(CH)]
        stats = [sb(f"stats{c}", [P, 6]) for c in range(CH)]
        moments = [sb(f"moments{c}", [P, 2]) for c in range(CH)]
        var_eps = [sb(f"var_eps{c}", [P, 1]) for c in range(CH)]
        rstd = [sb(f"rstd{c}", [P, 1]) for c in range(CH)]

        decay_ps = [pb(f"decay_ps{c}", [P, 2 * D]) for c in range(CH)]
        input_ps = [pb(f"input_ps{c}", [P, 2 * D]) for c in range(CH)]
        y_ps = [pb(f"y_ps{c}", [P, 2 * D]) for c in range(CH)]
        norm_ps = [pb(f"norm_ps{c}", [P, 2 * D]) for c in range(CH)]
        proj_ps = [decay_ps[0], decay_ps[1], input_ps[0], input_ps[1]]

        consts_in = sem("consts_in")
        x_in = sem("x_in")
        projected = sem("projected")
        c_projected = sem("c_projected")
        bias_added = sem("bias_added")
        c_copied = sem("c_copied")
        b_split = sem("b_split")
        b_stored = sem("b_stored")
        c_stored = sem("c_stored")
        b_loaded = sem("b_loaded")
        c_loaded = sem("c_loaded")
        b_widened = sem("b_widened")
        negated = sem("negated")
        softplus_ln = sem("softplus_ln")
        act_chain = sem("act_chain")
        dt_tanh = sem("dt_tanh")
        dt_done = sem("dt_done")
        dt_turned = sem("dt_turned")
        dt_cols_done = sem("dt_cols_done")
        v_split = sem("v_split")
        v_stored = sem("v_stored")
        v_loaded = sem("v_loaded")
        a_ready = sem("a_ready")
        pad_zeroed = sem("pad_zeroed")
        zeroed = sem("zeroed")
        dve_chain = sem("dve_chain")
        pool_chain = sem("pool_chain")
        z_low = sem("z_low")
        z_high = sem("z_high")
        c_spread = [sem(f"c_spread{c}") for c in range(CH)]
        x_skip_free = [sem(f"x_skip_free{c}") for c in range(CH)]
        tanh_done = sem("tanh_done")
        decay_done = sem("decay_done")
        decay_turned = [sem(f"decay_turned{c}") for c in range(CH)]
        input_done = [sem(f"input_done{c}") for c in range(CH)]
        h_done = [sem(f"h_done{c}") for c in range(CH)]
        decayed_done = [sem(f"decayed_done{c}") for c in range(CH)]
        squared = [sem(f"squared{c}") for c in range(CH)]
        normsq_done = [sem(f"normsq_done{c}") for c in range(CH)]
        clamped_done = [sem(f"clamped_done{c}") for c in range(CH)]
        scale_done = [sem(f"scale_done{c}") for c in range(CH)]
        scale_spread = [sem(f"scale_spread{c}") for c in range(CH)]
        rowscale_done = [sem(f"rowscale_done{c}") for c in range(CH)]
        rowscale_copied = [sem(f"rowscale_copied{c}") for c in range(CH)]
        residual_done = [sem(f"residual_done{c}") for c in range(CH)]
        y_step = [sem(f"y_step{c}") for c in range(CH)]
        y_taken = [sem(f"y_taken{c}") for c in range(CH)]
        xblk_in = [sem(f"xblk_in{c}") for c in range(CH)]
        xskip_done = [sem(f"xskip_done{c}") for c in range(CH)]
        stats_done = [sem(f"stats_done{c}") for c in range(CH)]
        moments_done = [sem(f"moments_done{c}") for c in range(CH)]
        var_done = [sem(f"var_done{c}") for c in range(CH)]
        rstd_done = [sem(f"rstd_done{c}") for c in range(CH)]
        normed_done = [sem(f"normed_done{c}") for c in range(CH)]
        x1_stored = [sem(f"x1_stored{c}") for c in range(CH)]

        block = ctx.enter_context(nc.Block())
        b_sets = [(0, 2), (2, 2), (4, 2), (6, 2)]

        @block.sync
        def _(sp):
            sp.dma_start(const[:, :], a["consts"]).then_inc(consts_in, 16)
            sp.dma_start(proj_w[:, :, :], a["projT"].rearrange("(h p) n -> p h n", p=P)).then_inc(consts_in, 16)
            sp.dma_start(x_cols[:, :].rearrange("p (h n) -> p h n", h=DH),
                         a["xT"].rearrange("(h p) n -> p h n", p=P)).then_inc(x_in, 16)
            sp.dma_start(bdt[:, :], a["L0_attn_bdt"].unsqueeze(0).broadcast_to([P, D])).then_inc(consts_in, 16)
            sp.dma_start(a_exp[:, :, :], a["L0_attn_A_log"].rearrange("(h p) n -> p h n", p=P)).then_inc(consts_in, 16)
            sp.dma_start(dp1[:, :], a["L0_attn_Dp"].unsqueeze(0).broadcast_to([P, D])).then_inc(consts_in, 16)
            sp.dma_start(x_rows.rearrange("p (j d) -> p j d", j=TILES),
                         a["x"].rearrange("b t d -> (b t) d").rearrange("(j p) d -> p j d", p=P)).then_inc(x_in, 16)
            sp.wait_ge(b_split, 3)
            for q in range(3):
                sp.dma_start(b_scratch[q].rearrange("(j p) n -> p j n", p=P),
                             b_pc[:, q, :].rearrange("p (j n) -> p j n", j=TILES)).then_inc(b_stored, 16)
            sp.wait_ge(c_copied, 4)
            sp.dma_start(c_scratch, c_rows).then_inc(c_stored, 16)
            sp.wait_ge(b_stored, 48)
            for r in range(COMBOS):
                sp.dma_start(b_rows[r * B:(r + 1) * B, :],
                             b_scratch[B_PIECE[r]].rearrange("(b t) n -> b (t n)", b=B)).then_inc(b_loaded, 16)
            sp.wait_ge(c_stored, 16)
            for b in range(B):
                sp.dma_start(c_col[(b % CB) * N:(b % CB + 1) * N, b // CB, :],
                             c_scratch[:, b * L:(b + 1) * L]).then_inc(c_loaded, 16)
            for q, piece in enumerate((v_hi, v_mid, v_lo)):
                sp.wait_ge(v_split, q + 1)
                sp.dma_start(v_scratch[q].rearrange("(j p) d -> p j d", p=P),
                             piece.rearrange("p (j d) -> p j d", j=TILES)).then_inc(v_stored, 16)
            sp.wait_ge(v_stored, 48)

            def load_v(start, size, at):
                for r in range(COMBOS):
                    sp.dma_start(v_rows[r * B:(r + 1) * B, bass.ds(at * D, size * D)],
                                 v_scratch[V_PIECE[r]].rearrange("(b t) d -> b (t d)", b=B)
                                 [:, bass.ds(start * D, size * D)]).then_inc(v_loaded, 16)

            load_v(0, TB, 0)
            for c in range(CH):
                sp.sem_inc(x1_stored[c], 16)

            def rows_of(dram, k, c):
                return dram[c * CB:(c + 1) * CB, bass.ds(k * TB, TB), :].rearrange("b t d -> t b d")

            def load_x_rows(k):
                for c in range(CH):
                    sp.wait_ge(xskip_done[c], k + 1)
                    sp.dma_start(x_blk[c], rows_of(a["x"], k, c))\
                        .then_inc(xblk_in[c], 16)

            def store_x1_rows(k):
                for c in range(CH):
                    sp.wait_ge(normed_done[c], k + 1)
                    sp.dma_start(rows_of(x1, k, c), normed[c])\
                        .then_inc(x1_stored[c], 16)

            def load_next_v(k):
                sp.wait_ge(v_loaded, 16 * COMBOS * (k + 1))
                load_v((k + 1) * TB, TB, (k + 1) * TB)

            load_x_rows(0)
            load_next_v(0)
            with nc.sync.Fori(1, BLOCKS - 1) as k:
                load_x_rows(k)
                load_next_v(k)
                store_x1_rows(k - 1)
            load_x_rows(BLOCKS - 1)
            sp.wait_ge(v_loaded, 16 * COMBOS * BLOCKS)
            load_v(0, 1, L)
            store_x1_rows(BLOCKS - 2)
            store_x1_rows(BLOCKS - 1)
            for c in range(CH):
                sp.wait_ge(x1_stored[c], 16 * BLOCKS + 16)

        @block.gpsimd
        def _(g):
            g.memset(minus_half[:, :], -0.5).then_inc(pool_chain, 1)
            g.memset(sixteenth[:, :], 1.0 / N).then_inc(pool_chain, 1)
            g.wait_ge(pool_chain, 2)
            for c in range(CH):
                g.sem_inc(xskip_done[c], 1)
                g.sem_inc(scale_done[c], 1)
                g.sem_inc(x_skip_free[c], 1)
            g.wait_ge(consts_in, 80)
            g.tensor_scalar(dp1[:, :], dp1[:, :], 1.0, None, ALU.add).then_inc(pool_chain, 1)
            g.wait_ge(pool_chain, 3)

            def half_of_decay_arguments(T, slot, c):
                g.wait_ge(decay_turned[c], T + 1)
                dt_col = dt_cols[:, 0, bass.ds(c * (CB * L) + T, CB, step=L)]
                g.tensor_tensor(ring[:, slot, 0, c, :].rearrange("p (b n) -> p b n", n=N),
                                dt_col.unsqueeze(2).broadcast_to([P, CB, N]),
                                a_exp[:, 0, :].unsqueeze(1).broadcast_to([P, CB, N]),
                                ALU.mult).then_inc(z_low, 1)

            def inverse_norm(T, s, c):
                g.wait_ge(clamped_done[c], T + 1)
                g.tensor_tensor(scale[c][:, s:s + 1], clamped[c][:, :], minus_half[:, :], ALU.pow)\
                    .then_inc(scale_done[c], 1)

            def spread_scales(k):
                for c in range(CH):
                    g.wait_ge(scale_done[c], k * TB + 1)
                    g.tensor_tensor(own_scale[c][:, :, :], scale[c][:, :].unsqueeze(2).broadcast_to([P, TB, CB]),
                                    own_batch.unsqueeze(1).broadcast_to([P, TB, CB]), ALU.mult)\
                        .then_inc(scale_spread[c], 1)

            def spread_c(k, c):
                g.wait_ge(y_step[c], k * TB + 2)
                g.tensor_tensor(turned_diagonal[c], c_col[:, c, bass.ds(k * TB, TB)].unsqueeze(2).broadcast_to([P, TB, CB]),
                                own_batch.unsqueeze(1).broadcast_to([P, TB, CB]), ALU.mult).then_inc(c_spread[c], 1)

            def block_steps(k, first):
                for s in range(TB):
                    T = k * TB + s
                    if s or not first:
                        inverse_norm(T - 1, (s - 1) % TB, 1)
                    if s == 0 and not first:
                        spread_scales(k)
                    half_of_decay_arguments(T + AHEAD, (s + AHEAD) % TB, 0)
                    if s == 0 and not first:
                        g.wait_ge(scale_spread[0], k)
                        g.wait_ge(scale_spread[1], k)
                    inverse_norm(T, s, 0)
                    half_of_decay_arguments(T + AHEAD, (s + AHEAD) % TB, 1)
                    if s in (4, 5):
                        c = s - 4
                        g.wait_ge(xblk_in[c], 16 * (k + 1))
                        g.wait_ge(x_skip_free[c], k + 1)
                        g.tensor_tensor(x_skip[c], x_blk[c], dp1[:, :], ALU.mult).then_inc(xskip_done[c], 1)
                    if s in (10, 11) and not first:
                        inverse_deviation(k, s - 10)

            def inverse_deviation(k, c):
                g.wait_ge(var_done[c], k)
                g.tensor_tensor(rstd[c][:, :], var_eps[c][:, :], minus_half[:, :], ALU.pow).then_inc(rstd_done[c], 1)

            g.wait_ge(a_ready, 2)
            g.wait_ge(dt_cols_done, TILES)
            g.wait_ge(pad_zeroed, 1)
            g.wait_ge(v_split, 3)
            for T in range(AHEAD):
                for c in range(CH):
                    half_of_decay_arguments(T, T, c)
            g.wait_ge(c_loaded, 16 * B)
            g.wait_ge(v_stored, 48)
            g.memset(turned_c[:, :], 0.0).then_inc(pool_chain, 1)
            g.wait_ge(pool_chain, 4)
            for c in range(CH):
                spread_c(0, c)
            block_steps(0, True)
            with nc.gpsimd.Fori(1, BLOCKS) as k:
                for c in range(CH):
                    spread_c(k, c)
                block_steps(k, False)
            inverse_norm(L - 1, TB - 1, 1)
            spread_scales(BLOCKS)
            for c in range(CH):
                inverse_deviation(BLOCKS, c)

        @block.scalar
        def _(act):
            act.wait_ge(negated, 1)
            act.activation(v_work, v_work, ACT.Exp).then_inc(act_chain, 1)
            act.wait_ge(consts_in, 80)
            act.wait_ge(act_chain, 1)
            act.activation(v_work, v_work, ACT.Ln, bias=1.0).then_inc(softplus_ln, 1)
            act.activation(a_exp[:, :, :], a_exp[:, :, :], ACT.Tanh, scale=0.5 / (5.0 + 1e-8)).then_inc(a_ready, 1)
            act.wait_ge(a_ready, 1)
            act.activation(a_exp[:, :, :], a_exp[:, :, :], ACT.Exp, scale=10.0).then_inc(a_ready, 1)
            act.wait_ge(dt_done, 1)
            act.activation(dt_rows, dt_rows, ACT.Tanh, bias=tanh_bias[:, :],
                           scale=0.5 / (DT_R + 1e-8)).then_inc(dt_tanh, 1)
            for j in range(TILES):
                act.wait_ge(dt_turned, j + 1)
                act.activation(dt_cols[:, :, j * P:(j + 1) * P],
                               proj_ps[j % 4][:, 0:DH * P].rearrange("p (h n) -> p h n", h=DH), ACT.Copy)\
                    .then_inc(dt_cols_done, 1)

            def decay_tanh(T, slot):
                act.wait_ge(z_low, (T + 1) * CH)
                act.wait_ge(z_high, T + 1)
                act.activation(ring[:, slot], ring[:, slot], ACT.Tanh, scale=-0.5 / (8.0 + 1e-8)).then_inc(tanh_done, 1)

            def decay_exp(T, slot):
                act.wait_ge(tanh_done, T + 1)
                act.activation(ring[:, slot], ring[:, slot], ACT.Exp, scale=16.0).then_inc(decay_done, 1)

            def square(T, s, c):
                act.wait_ge(h_done[c], T + 1)
                act.activation(squares[c], h[c][s % 2], ACT.Square, scale=1.0 / CLAMP,
                               accum_out=sumsq[c][:, :]).then_inc(squared[c], 1)

            for T in range(AHEAD - 1):
                decay_tanh(T, T)
                decay_exp(T, T)
            with nc.scalar.Fori(0, BLOCKS) as k:
                for s in range(TB):
                    T = k * TB + s
                    square(T, s, 0)
                    decay_tanh(T + AHEAD - 1, (s + AHEAD - 1) % TB)
                    square(T, s, 1)
                    decay_exp(T + AHEAD - 1, (s + AHEAD - 1) % TB)

        @block.tensor
        def _(pe):
            pe.wait_ge(consts_in, 80)
            pe.wait_ge(x_in, 32)
            xc = x_cols[:, :].rearrange("p (h n) -> p h n", h=DH)
            for j in range(TILES):
                if j >= 4:
                    pe.wait_ge(bias_added, j - 3)
                for hf in range(DH):
                    mm = pe.matmul(proj_ps[j % 4][:, 0:D + N], xc[:, hf, j * P:(j + 1) * P],
                                   proj_w[:, hf, 0:D + N], start=(hf == 0), stop=(hf == DH - 1))
                mm.then_inc(projected, 1)
            q = TOK // 4
            for j in range(4):
                for hf in range(DH):
                    mm = pe.matmul((y_ps + norm_ps)[j][0:N, 0:q], proj_w[:, hf, D + N:D + 2 * N],
                                   xc[:, hf, j * q:(j + 1) * q], start=(hf == 0), stop=(hf == DH - 1))
                mm.then_inc(c_projected, 1)
            pe.wait_ge(dt_done, 2)
            pe.wait_ge(bias_added, TILES)
            for j in range(TILES):
                if j >= 4:
                    pe.wait_ge(dt_cols_done, j - 3)
                for hf in range(DH):
                    mm = pe.transpose(proj_ps[j % 4][:, hf * P:(hf + 1) * P],
                                      dt_rows[:, j * D + hf * P:j * D + (hf + 1) * P], ident)
                mm.then_inc(dt_turned, 1)
            for c in range(CH):
                pe.sem_inc(decay_turned[c], 1 + AHEAD)
                pe.sem_inc(y_step[c], 2)

            def turn_decay(T, s, c):
                pe.wait_ge(decay_done, T + 1)
                for hf in range(DH):
                    mm = pe.transpose(decay_ps[c][:, hf * P:(hf + 1) * P],
                                      ring[:, s % TB, hf, c, :], ident)
                mm.then_inc(decay_turned[c], 1)

            def input_product(T, s, c):
                pe.matmul(input_ps[c][:, 0:D], b_wide[c][:, bass.ds(T * P, P)],
                          v_rows[:, bass.ds(T * D, D)], start=True, stop=True).then_inc(input_done[c], 1)

            def norm_product(T, c):
                pe.wait_ge(squared[c], T + 1)
                pe.matmul(norm_ps[c][:, 0:1], block_ones, sumsq[c][:, :], start=True, stop=True)\
                    .then_inc(normsq_done[c], 1)

            def output_product(T, k, s, c):
                if s == 0:
                    pe.wait_ge(y_taken[c], k + 1)
                    pe.wait_ge(c_spread[c], k + 1)
                pe.matmul(y_ps[c][:, 0:D], turned_set[c][:, s * P:(s + 1) * P],
                          h[c][s % 2], start=(s == 0), stop=(s == TB - 1)).then_inc(y_step[c], 1)

            def row_scale_product(k, c):
                pe.wait_ge(scale_spread[c], k)
                pe.matmul(norm_ps[c][:, 1:2], own_scale[c][:, :, :].rearrange("p t b -> p (t b)"),
                          sixteenth[:, :], start=True, stop=True).then_inc(rowscale_done[c], 1)

            def block_steps(k, first):
                for s in range(TB):
                    T = k * TB + s
                    if s == TB - 1:
                        pe.wait_ge(v_loaded, 16 * COMBOS * (k + 2))
                    for c in range(CH):
                        pe.wait_ge(h_done[c], T + 1)
                        input_product(T + 1, s + 1, c)
                        output_product(T, k, s, c)
                        if s == 1 and not first:
                            pe.wait_ge(squared[c], T + 1)
                            row_scale_product(k, c)
                        norm_product(T, c)
                        pe.wait_ge(decayed_done[c], T + 3)
                        turn_decay(T + 2, s + 2, c)

            pe.wait_ge(dt_cols_done, TILES)
            pe.wait_ge(b_widened, B)
            pe.wait_ge(zeroed, 3)
            for c in range(CH):
                pe.wait_ge(v_loaded, 16 * COMBOS)
                input_product(0, 0, c)
                turn_decay(1, 1, c)
            block_steps(0, True)
            with nc.tensor.Fori(1, BLOCKS) as k:
                block_steps(k, False)
            for c in range(CH):
                pe.wait_ge(clamped_done[c], L)
                row_scale_product(BLOCKS, c)

        @block.vector
        def _(dve):
            count = [0]

            def chained(ins):
                count[0] += 1
                ins.then_inc(dve_chain, 1)
                dve.wait_ge(dve_chain, count[0])

            dve.memset(tanh_bias[:, :], -DT_C * 0.5 / (DT_R + 1e-8)).then_inc(zeroed, 1)
            for c in range(CH):
                dve.memset(decayed[c][:, :], 0.0).then_inc(decayed_done[c], 1)
                dve.memset(scale[c][:, TB - 1:TB], 1.0).then_inc(decayed_done[c], 1)
            dve.memset(dt_cols[:, :, TOK:TOK + AHEAD], 0.0).then_inc(pad_zeroed, 1)
            for c in range(CH):
                dve.memset(b_wide[c][:, L * P:(L + 1) * P], 0.0).then_inc(zeroed, 1)
            dve.wait_ge(consts_in, 80)
            for j in range(TILES):
                dve.wait_ge(projected, j + 1)
                dve.tensor_copy(bc[:, j * N:(j + 1) * N], proj_ps[j % 4][:, D:D + N])
                dve.tensor_tensor(dt_rows[:, j * D:(j + 1) * D], proj_ps[j % 4][:, 0:D], bdt[:, :], ALU.add)\
                    .then_inc(bias_added, 1)
            dve.wait_ge(bias_added, TILES)
            chained(dve.tensor_scalar(v_work, dt_rows, -1.0, None, ALU.mult))
            dve.tensor_tensor(v_work, v_work, dt_rows, ALU.min).then_inc(negated, 1)
            dve.tensor_copy(b_pc[:, 0, :], bc).then_inc(b_split, 1)
            dve.wait_ge(b_split, 1)
            chained(dve.tensor_tensor(b_work, bc, b_pc[:, 0, :], ALU.subtract))
            dve.tensor_copy(b_pc[:, 1, :], b_work).then_inc(b_split, 1)
            dve.wait_ge(b_split, 2)
            dve.tensor_tensor(b_pc[:, 2, :], b_work, b_pc[:, 1, :], ALU.subtract).then_inc(b_split, 1)
            for j in range(4):
                dve.wait_ge(c_projected, j + 1)
                dve.tensor_copy(c_rows[:, j * (TOK // 4):(j + 1) * (TOK // 4)],
                                (y_ps + norm_ps)[j][0:N, 0:TOK // 4]).then_inc(c_copied, 1)
            dve.wait_ge(softplus_ln, 1)
            dve.scalar_tensor_tensor(out=dt_rows, in0=dt_rows, scalar=0.0, in1=v_work,
                                     op0=ALU.max, op1=ALU.add).then_inc(dt_done, 1)
            dve.wait_ge(dt_tanh, 1)
            dve.tensor_scalar(dt_rows, dt_rows, 2.0 * DT_R, DT_C, ALU.mult, ALU.add).then_inc(dt_done, 1)
            dve.wait_ge(dt_done, 2)
            dve.wait_ge(x_in, 32)
            chained(dve.tensor_tensor(v_work, dt_rows, x_rows, ALU.mult))
            dve.wait_ge(c_projected, 4)
            dve.tensor_copy(v_hi, v_work).then_inc(v_split, 1)
            dve.wait_ge(v_split, 1)
            chained(dve.tensor_tensor(v_work, v_work, v_hi, ALU.subtract))
            dve.tensor_copy(v_mid, v_work).then_inc(v_split, 1)
            dve.wait_ge(v_split, 2)
            dve.tensor_tensor(v_lo, v_work, v_mid, ALU.subtract).then_inc(v_split, 1)
            dve.wait_ge(b_loaded, 16 * COMBOS)
            for b in range(B):
                dve.tensor_scalar(b_wide[b // CB][:, 0:L * P].rearrange("p (t b n) -> p t b n", b=CB, n=N)[:, :, b % CB, :],
                                  b_rows[:, :].rearrange("p (t n) -> p t n", n=N),
                                  row_batch[:, b:b + 1], None, ALU.mult).then_inc(b_widened, 1)
            for c in range(CH):
                dve.sem_inc(y_taken[c], 1)

            def state(T, s, c):
                dve.wait_ge(input_done[c], T + 1)
                dve.wait_ge(scale_done[c], T + 1)
                dve.wait_ge(decayed_done[c], T + 2)
                dve.wait_ge(y_step[c], T + 1)
                dve.scalar_tensor_tensor(out=h[c][s % 2], in0=decayed[c][:, :], scalar=scale[c][:, (s - 1) % TB:(s - 1) % TB + 1],
                                         in1=input_ps[c][:, 0:D],
                                         op0=ALU.mult, op1=ALU.add).then_inc(h_done[c], 1)

            def decay(T, s, c):
                dve.wait_ge(h_done[c], T + 1)
                dve.wait_ge(decay_turned[c], AHEAD + T + 2)
                dve.tensor_tensor(decayed[c][:, :], h[c][s % 2], decay_ps[c][:, 0:D], ALU.mult)\
                    .then_inc(decayed_done[c], 1)

            def clamp_norm(T, c):
                dve.wait_ge(normsq_done[c], T + 1)
                dve.tensor_scalar(clamped[c][:, :], norm_ps[c][:, 0:1], 1.0, 2e-8 / CLAMP, ALU.max, ALU.add)\
                    .then_inc(clamped_done[c], 1)

            def half_of_decay_arguments(T, slot):
                for c in range(CH):
                    dve.wait_ge(decay_turned[c], T + 1)
                dve.tensor_tensor(ring[:, slot, 1, :, :].rearrange("p c (b n) -> p (c b) n", n=N),
                                  dt_cols[:, 1, bass.ds(T, B, step=L)].unsqueeze(2).broadcast_to([P, B, N]),
                                  a_exp[:, 1, :].unsqueeze(1).broadcast_to([P, B, N]),
                                  ALU.mult).then_inc(z_high, 1)

            def take_outputs(k, c):
                dve.wait_ge(y_step[c], k * TB + TB + 2)
                dve.wait_ge(x_skip_free[c], k + 1)
                dve.tensor_copy(y_rows[c][:, :], y_ps[c][:, 0:D]).then_inc(y_taken[c], 1)

            def take_row_scale(k, c):
                dve.wait_ge(rowscale_done[c], k)
                dve.tensor_copy(row_scale[c][:, :], norm_ps[c][:, 1:2]).then_inc(rowscale_copied[c], 1)

            def residual(k, c):
                dve.wait_ge(rowscale_copied[c], k)
                dve.wait_ge(y_taken[c], k + 1)
                dve.wait_ge(xskip_done[c], k + 1)
                dve.scalar_tensor_tensor(out=res[c], in0=y_rows[c][:, :], scalar=row_scale[c][:, :], in1=x_skip[c],
                                         op0=ALU.mult, op1=ALU.add).then_inc(x_skip_free[c], 1)

            def statistics(k, c):
                dve.wait_ge(x_skip_free[c], k + 1)
                dve.bn_stats(stats[c][:, :], res[c]).then_inc(stats_done[c], 1)

            def aggregate(c):
                dve.bn_aggr(moments[c][:, :], stats[c][:, :]).then_inc(moments_done[c], 1)

            def variance(k, c):
                dve.wait_ge(moments_done[c], k)
                dve.tensor_scalar(var_eps[c][:, :], moments[c][:, 1:2], EPS, None, ALU.add).then_inc(var_done[c], 1)

            def normalise(k, c):
                dve.wait_ge(rstd_done[c], k)
                dve.wait_ge(x1_stored[c], 16 * k)
                dve.tensor_scalar(normed[c], res[c], moments[c][:, 0:1], rstd[c][:, :],
                                  ALU.subtract, ALU.mult).then_inc(normed_done[c], 1)

            def block_steps(k, first):
                for s in range(TB):
                    T = k * TB + s
                    if s in (6, 7) and not first:
                        dve.wait_ge(stats_done[s - 6], k)
                    state(T, s, 0)
                    if s or not first:
                        clamp_norm(T - 1, 1)
                    if s == 2 and not first:
                        take_row_scale(k, 1)
                    decay(T, s, 0)
                    half_of_decay_arguments(T + AHEAD, (s + AHEAD) % TB)
                    state(T, s, 1)
                    clamp_norm(T, 0)
                    if s == 1 and not first:
                        take_row_scale(k, 0)
                    decay(T, s, 1)
                    if s == TB - 1:
                        take_outputs(k, 0)
                        take_outputs(k, 1)
                    if not first:
                        if s in (2, 3):
                            residual(k, s - 2)
                        if s in (4, 5):
                            statistics(k, s - 4)
                        if s in (6, 7):
                            aggregate(s - 6)
                        if s in (8, 9):
                            variance(k, s - 8)
                        if s in (12, 13):
                            normalise(k, s - 12)

            dve.wait_ge(v_split, 3)
            dve.wait_ge(dt_cols_done, TILES)
            dve.wait_ge(a_ready, 2)
            for T in range(AHEAD):
                half_of_decay_arguments(T, T)
            block_steps(0, True)
            with nc.vector.Fori(1, BLOCKS) as k:
                block_steps(k, False)
            clamp_norm(L - 1, 1)
            for c in range(CH):
                take_row_scale(BLOCKS, c)
            for c in range(CH):
                residual(BLOCKS, c)
            for c in range(CH):
                statistics(BLOCKS, c)
            for c in range(CH):
                dve.wait_ge(stats_done[c], BLOCKS)
                aggregate(c)
            for c in range(CH):
                variance(BLOCKS, c)
            for c in range(CH):
                normalise(BLOCKS, c)


S = 375
SK = 3
SC = S // SK
F = 1024
FC = F // P
PAIRS = B // 2
GATES = 3
GROUP = 4
SCORE = 1.0 / 16.0


def decoder_and_cell(nc, used, a, x1, out):
    with ExitStack() as ctx:
        def sb(name, shape, dt=F32):
            return ctx.enter_context(nc.sbuf_tensor(name, shape, dt))

        def sb2(name, shape, dt=F32):
            return [sb(f"{name}{j}", shape, dt) for j in range(2)]

        def pb(name):
            return ctx.enter_context(nc.psum_tensor(name, [P, 512], F32))

        def sem(name):
            used.append(nc.alloc_semaphore(name))
            return used[-1]

        def sem2(name):
            return [sem(f"{name}{j}") for j in range(2)]

        const = sb("const_b", [P, a["consts"].shape[1]])
        ident = const[:, 0:P]
        ident_l = const[0:L, 0:L]
        causal = const[0:L, 2 * P + CB + B:2 * P + CB + B + L]
        w1 = sb("w1", [P, DH, F])
        w2 = sb("w2", [P, FC, D])
        gate_w = sb("gate_w", [P, DH, 2, 4, D])
        vectors = sb("vectors", [P, FC + GATES * DH + DH])
        b1 = vectors[:, 0:FC]
        gate_b = vectors[:, FC:FC + GATES * DH].rearrange("p (g h) -> p g h", g=GATES)
        in_c = vectors[:, FC + GATES * DH:FC + GATES * DH + DH]
        norm_w = sb("norm_w", [L, 8, D])
        minus_half = sb("minus_half_b", [P, GROUP])
        ones_l = sb("ones_l", [P, L])
        spare = sb("spare", [P, 1])
        x1_att = sb2("x1_att", [L, D])
        x1_res = sb2("x1_res", [L, D])
        x1_cols = sb2("x1_cols", [P, DH, L])
        self_s = sb2("self_s", [L, L])
        self_p = sb2("self_p", [L, L])
        self_pt = sb2("self_pt", [L, L])
        ctx_cols = sb2("ctx_cols", [P, DH, S])
        ctx_rows = sb2("ctx_rows", [SC, SK, D])
        cross_p = sb2("cross_p", [L, S])
        cross_pt = sb2("cross_pt", [SC, SK, L])
        neg_max = [sb2(f"neg_max{i}", [L, 1]) for i in range(2)]
        row_max = [sb2(f"row_max{i}", [L, 1]) for i in range(2)]
        row_sum = [sb2(f"row_sum{i}", [L, 1]) for i in range(2)]
        inv_sum = [sb2(f"inv_sum{i}", [L, 1]) for i in range(2)]
        ln_in = [sb2(f"ln_in{i}", [L, D]) for i in range(4)]
        ln_out = [sb2(f"ln_out{i}", [L, D]) for i in range(2)]
        ln_stats = [sb2(f"ln_stats{i}", [L, 6]) for i in range(4)]
        ln_mv = [sb2(f"ln_mv{i}", [L, 2]) for i in range(4)]
        ln_var = [sb2(f"ln_var{i}", [L, 1]) for i in range(4)]
        ln_rstd = [sb2(f"ln_rstd{i}", [L, 1]) for i in range(4)]
        y1_cols = sb2("y1_cols", [P, DH, L])
        y2_bias = sb2("y2_bias", [L, D])
        y2_cols = sb("y2_cols", [P, DH, 2, L])
        hidden = sb("hidden", [P, FC, 2, L])
        x2_cols = sb2("x2_cols", [P, DH, L])
        fresh = sb2("fresh", [L, 2, D])
        all_rows = sb("all_rows", [L, 2, B, D])
        x2_all, wo_all = all_rows[:, 0, :, :], all_rows[:, 1, :, :]
        gate_t = sb("gate_t", [P, GATES, DH, L])
        cell2 = sb("cell2", [P, DH, L])
        kept = sb("kept", [P, DH, L])
        added = sb("added", [P, DH, L])
        base = sb("base", [L, D])
        fin_stats = sb("fin_stats", [L, B, 6])
        fin_mv = sb("fin_mv", [L, B, 2])
        fin_var = sb("fin_var", [L, B])
        fin_rstd = sb("fin_rstd", [L, B])

        att_ps = [pb(f"att_ps{j}") for j in range(2)]
        ff1_ps = [pb(f"ff1_ps{i}") for i in range(2)]
        ff2_ps = [pb(f"ff2_ps{j}") for j in range(2)]
        gate_ps = [pb(f"gate_ps{i}") for i in range(2)]

        small_in = sem("small_in")
        w_in = sem("w_in")
        n_in = sem("n_in")
        setup = sem("setup")
        gate_b_halved = sem("gate_b_halved")
        u_halved = sem("u_halved")
        ones_done = sem("ones_done")
        x1_in, x1r_in, ctx_in = sem2("x1_in"), sem2("x1r_in"), sem2("ctx_in")
        x1_turned, x1_cols_done = sem2("x1_turned"), sem2("x1_cols_done")
        self_scored, self_masked, self_max, self_neg, self_exp = (
            sem2("self_scored"), sem2("self_masked"), sem2("self_max"), sem2("self_neg"), sem2("self_exp"))
        self_inv, self_turned, self_pt_done, self_mixed = (
            sem2("self_inv"), sem2("self_turned"), sem2("self_pt_done"), sem2("self_mixed"))
        y1_turned, y1_cols_done = sem2("y1_turned"), sem2("y1_cols_done")
        cross_scored, cross_max, cross_neg, cross_exp = (
            sem2("cross_scored"), sem2("cross_max"), sem2("cross_neg"), sem2("cross_exp"))
        cross_inv, cross_turned, cross_pt_done, cross_mixed = (
            sem2("cross_inv"), sem2("cross_turned"), sem2("cross_pt_done"), sem2("cross_mixed"))
        y2_turned, y2_cols_done, y2_bias_done = sem2("y2_turned"), sem2("y2_cols_done"), sem2("y2_bias_done")
        ff1_done, hidden_done = sem("ff1_done"), sem("hidden_done")
        ff2_done = sem2("ff2_done")
        ln_summed = [sem2(f"ln_summed{i}") for i in range(4)]
        ln_stat = [sem2(f"ln_stat{i}") for i in range(4)]
        ln_agg = [sem2(f"ln_agg{i}") for i in range(4)]
        ln_vared = [sem2(f"ln_vared{i}") for i in range(4)]
        ln_rooted = [sem2(f"ln_rooted{i}") for i in range(4)]
        ln_centred = [sem2(f"ln_centred{i}") for i in range(3)]
        ln_done = [sem2(f"ln_done{i}") for i in (0, 1)]
        x2_done = sem2("x2_done")
        x1_beta_done = sem2("x1_beta_done")
        x2_turned, x2_cols_done, rows_kept = sem2("x2_turned"), sem2("x2_cols_done"), sem2("rows_kept")
        wo_done, wo_copied = sem2("wo_done"), sem2("wo_copied")
        gates_done, gates_tanh = sem("gates_done"), sem("gates_tanh")
        cell_kept, cell_added, cell_done = sem("cell_kept"), sem("cell_added"), sem("cell_done")
        u_done, base_done = sem("u_done"), sem("base_done")
        fin_arg, fin_tanh, fin_sum, fin_stat, fin_agg, fin_vared, fin_rooted, fin_normed = (
            sem("fin_arg"), sem("fin_tanh"), sem("fin_sum"), sem("fin_stat"), sem("fin_agg"), sem("fin_vared"),
            sem("fin_rooted"), sem("fin_normed"))
        out_stored = sem("out_stored")

        def after(eng, s, count):
            if not (isinstance(count, int) and count <= 0):
                eng.wait_ge(s, count)

        block = ctx.enter_context(nc.Block())

        @block.sync
        def _(sp):
            def pair_of(dram, p, j):
                return dram.rearrange("(p j) r c -> p j r c", j=2)[bass.ds(p, 1), j]

            def kept_rows(q, j):
                return all_rows[:, :, :, :].rearrange("t w (p j) d -> t w p j d", j=2)[:, :, bass.ds(q, 1), j, :]\
                    .rearrange("t w b d -> t w (b d)")

            def load_rows(p, first=False):
                for j in range(2):
                    if not first:
                        sp.wait_ge(self_mixed[j], p)
                        sp.wait_ge(ln_summed[0][j], p)
                    sp.dma_start(x1_att[j][:, :], pair_of(x1, p, j).rearrange("b t d -> (b t) d"))\
                        .then_inc(x1_in[j], 16)

            def load_context(p, first=False):
                for j in range(2):
                    if not first:
                        sp.wait_ge(cross_mixed[j], p)
                    sp.dma_start(ctx_cols[j][:, :, :],
                                 pair_of(a["ctxT"], p, j).rearrange("b (h p) s -> p (b h) s", p=P))\
                        .then_inc(ctx_in[j], 16)
                    sp.dma_start(ctx_rows[j][:, :, :],
                                 pair_of(a["ctx_1024"], p, j).rearrange("b (k s) d -> s (b k) d", s=SC))\
                        .then_inc(ctx_in[j], 16)

            def load_residual(q, first=False):
                for j in range(2):
                    if not first:
                        sp.wait_ge(ln_summed[3][j], q)
                    sp.dma_start(x1_res[j][:, :], pair_of(x1, q, j).rearrange("b t d -> (b t) d"))\
                        .then_inc(x1r_in[j], 16)

            def keep(q):
                for j in range(2):
                    sp.wait_ge(wo_copied[j], q + 2)
                    sp.dma_start(kept_rows(q, j), fresh[j][:, :, :]).then_inc(rows_kept[j], 16)

            sp.dma_start(const[:, :], a["consts"]).then_inc(small_in, 16)
            load_rows(0, True)
            sp.dma_start(vectors[:, :], a["vectors"]).then_inc(small_in, 16)
            load_context(0, True)
            load_residual(0, True)
            sp.dma_start(w1[:, :, :], a["L0_xattn_w1"].rearrange("(h p) f -> p h f", p=P)).then_inc(w_in, 16)
            sp.dma_start(w2[:, :, :], a["L0_xattn_w2"].rearrange("(c p) d -> p c d", p=P)).then_inc(w_in, 16)
            sp.dma_start(gate_w[:, :, :, :, :], a["gateT"].rearrange("(h p) (w g n) -> p h w g n", p=P, w=2, g=4))\
                .then_inc(w_in, 16)
            load_rows(1)
            load_context(1)
            with nc.sync.Fori(1, PAIRS - 1) as p:
                load_rows(p + 1)
                load_residual(p)
                load_context(p + 1)
                keep(p - 1)
            load_residual(PAIRS - 1)
            keep(PAIRS - 2)
            keep(PAIRS - 1)
            for g in range(B // GROUP):
                sp.wait_ge(fin_normed, GROUP * (g + 1))
                sp.dma_start(out[g * GROUP:(g + 1) * GROUP].rearrange("b t d -> t b d"),
                             x2_all[:, g * GROUP:(g + 1) * GROUP, :]).then_inc(out_stored, 16)
            sp.wait_ge(out_stored, 16 * (B // GROUP))

        @block.gpsimd
        def _(g):
            def root(i, p, j):
                g.wait_ge(ln_vared[i][j], p + 1)
                g.tensor_tensor(ln_rstd[i][j][:, :], ln_var[i][j][:, :], minus_half[0:L, 0:1], ALU.pow)\
                    .then_inc(ln_rooted[i][j], 1)

            def add_b2(p, j):
                g.wait_ge(ln_done[1][j], p + 1)
                g.tensor_tensor(y2_bias[j][:, :], ln_out[1][j][:, :], norm_w[:, 6, :], ALU.add)\
                    .then_inc(y2_bias_done[j], 1)

            def add_beta3(q, j):
                g.wait_ge(x1r_in[j], 16 * (q + 1))
                g.tensor_tensor(x1_res[j][:, :], x1_res[j][:, :], norm_w[:, 5, :], ALU.add)\
                    .then_inc(x1_beta_done[j], 1)

            def pair_step(p, q):
                if q is not None:
                    add_beta3(q, 0)
                    add_beta3(q, 1)
                if p is not None:
                    root(0, p, 0)
                    root(0, p, 1)
                if q is not None:
                    for j in range(2):
                        root(2, q, j)
                        root(3, q, j)
                if p is not None:
                    for j in range(2):
                        root(1, p, j)
                    for j in range(2):
                        add_b2(p, j)

            for i, n in enumerate(("g1", "beta1", "g2", "beta2", "g3", "beta3", "b2")):
                g.dma_start(norm_w[:, i, :], a[f"L0_xattn_{n}"].unsqueeze(0).broadcast_to([L, D])).then_inc(n_in, 16)
            g.dma_start(norm_w[:, 7, :], a["L0_ffn_bo"].unsqueeze(0).broadcast_to([L, D])).then_inc(n_in, 16)
            g.memset(minus_half[:, :], -0.5).then_inc(setup, 1)
            g.wait_ge(setup, 1)
            g.wait_ge(n_in, 128)
            pair_step(0, None)
            with nc.gpsimd.Fori(1, PAIRS) as p:
                pair_step(p, p - 1)
            pair_step(None, PAIRS - 1)
            for q in range(B // GROUP):
                g.wait_ge(fin_vared, q + 1)
                g.tensor_tensor(fin_rstd[:, q * GROUP:(q + 1) * GROUP], fin_var[:, q * GROUP:(q + 1) * GROUP],
                                minus_half[0:L, :], ALU.pow).then_inc(fin_rooted, 1)

        @block.scalar
        def _(act):
            def copy(dst, src, done):
                act.activation(dst, src, ACT.Copy).then_inc(done, 1)

            def columns(ps):
                return ps[:, 0:DH * L].rearrange("p (h t) -> p h t", h=DH)

            def relu(q, u):
                act.wait_ge(ff1_done, q * (FC // 2) + u + 1)
                for i in range(2):
                    c = 2 * u + i
                    act.activation(hidden[:, c, :, :].rearrange("p j t -> p (j t)"),
                                   ff1_ps[u % 2][:, i * 2 * L:(i + 1) * 2 * L], ACT.Relu, bias=b1[:, c:c + 1])\
                        .then_inc(hidden_done, 1)

            def gate_tanh(q, j):
                act.wait_ge(gates_done, 2 * q + j + 1)
                for g in range(GATES):
                    for hf in range(DH):
                        ps = gate_ps[g // 2][:, ((g % 2) * DH + hf) * L:((g % 2) * DH + hf + 1) * L]
                        act.activation(gate_t[:, g, hf, :], ps, ACT.Tanh, bias=gate_b[:, g, hf:hf + 1],
                                       scale=0.5 if g < 2 else 1.0).then_inc(gates_tanh, 1)

            def copy_x2(q, j):
                act.wait_ge(x2_turned[j], q + 1)
                copy(x2_cols[j][:, :, :], columns(ff2_ps[j]), x2_cols_done[j])

            def copy_wo(q, j):
                act.wait_ge(wo_done[j], q + 1)
                act.wait_ge(rows_kept[j], 16 * (q + 1))
                copy(fresh[j][:, 1, :], ff2_ps[j][0:L, 0:D], wo_copied[j])

            def columns_of(turned, cols, done, p):
                for j in range(2):
                    act.wait_ge(turned[j], p + 1)
                    copy(cols[j], columns(att_ps[j]), done[j])

            def cross_exponent(p, j):
                act.wait_ge(cross_neg[j], p + 1)
                act.activation(cross_p[j][:, :], att_ps[j][0:L, 0:S], ACT.Exp, bias=neg_max[1][j][:, :],
                               scale=SCORE, accum_out=row_sum[1][j][:, :]).then_inc(cross_exp[j], 1)

            def pair_step(p, q):
                if p is not None:
                    columns_of(x1_turned, [t[:, :, :] for t in x1_cols], x1_cols_done, p)
                if q is not None:
                    relu(q, 0)
                    relu(q, 1)
                if p is not None:
                    for j in range(2):
                        act.wait_ge(self_neg[j], p + 1)
                        act.activation(self_p[j][:, :], self_s[j][:, :], ACT.Exp, bias=neg_max[0][j][:, :],
                                       accum_out=row_sum[0][j][:, :]).then_inc(self_exp[j], 1)
                if q is not None:
                    relu(q, 2)
                if p is not None:
                    for j in range(2):
                        act.wait_ge(self_turned[j], p + 1)
                        copy(self_pt[j][:, :], att_ps[j][0:L, 0:L], self_pt_done[j])
                if q is not None:
                    relu(q, 3)
                if p is not None:
                    columns_of(y1_turned, [t[:, :, :] for t in y1_cols], y1_cols_done, p)
                    cross_exponent(p, 0)
                if q is not None:
                    copy_x2(q, 0)
                if p is not None:
                    cross_exponent(p, 1)
                if q is not None:
                    gate_tanh(q, 0)
                if p is not None:
                    for j in range(2):
                        act.wait_ge(cross_turned[j], p + 1)
                        copy(cross_pt[j][:, :, :], att_ps[j][0:SC, 0:SK * L].rearrange("p (k t) -> p k t", k=SK),
                             cross_pt_done[j])
                if q is not None:
                    copy_wo(q, 0)
                    copy_x2(q, 1)
                    gate_tanh(q, 1)
                    copy_wo(q, 1)
                if p is not None:
                    columns_of(y2_turned, [y2_cols[:, :, j, :] for j in range(2)], y2_cols_done, p)

            for j in range(2):
                act.sem_inc(wo_copied[j], 1)
            act.wait_ge(small_in, 32)
            act.wait_ge(gate_b_halved, 1)
            pair_step(0, None)
            with nc.scalar.Fori(1, PAIRS) as p:
                pair_step(p, p - 1)
            pair_step(None, PAIRS - 1)
            for q in range(B // GROUP):
                act.wait_ge(fin_arg, q + 1)
                t = wo_all[:, q * GROUP:(q + 1) * GROUP, :]
                act.activation(t, t, ACT.Tanh).then_inc(fin_tanh, 1)

        @block.tensor
        def _(pe):
            def turn(ps, rows, width, done, src, identity):
                for i in range(width // P):
                    mm = pe.transpose(ps[:, i * L:i * L + L], src[:, i * P:(i + 1) * P], identity)
                mm.then_inc(done, 1)

            def self_turn_x1(p, j):
                pe.wait_ge(x1_in[j], 16 * (p + 1))
                after(pe, y2_cols_done[j], p)
                turn(att_ps[j], L, D, x1_turned[j], x1_att[j], ident_l)

            def self_scores(p, j):
                pe.wait_ge(x1_cols_done[j], p + 1)
                for hf in range(DH):
                    mm = pe.matmul(att_ps[j][0:L, 0:L], x1_cols[j][:, hf, :], x1_cols[j][:, hf, :],
                                   start=(hf == 0), stop=(hf == DH - 1))
                mm.then_inc(self_scored[j], 1)

            def self_turn(p, j):
                pe.wait_ge(self_exp[j], p + 1)
                pe.transpose(att_ps[j][0:L, 0:L], self_p[j][:, :], ident_l).then_inc(self_turned[j], 1)

            def self_mix(p, j):
                pe.wait_ge(self_pt_done[j], p + 1)
                pe.matmul(att_ps[j][0:L, 0:D], self_pt[j][:, :], x1_att[j][:, :], start=True, stop=True)\
                    .then_inc(self_mixed[j], 1)

            def turn_y1(p, j):
                pe.wait_ge(ln_done[0][j], p + 1)
                turn(att_ps[j], L, D, y1_turned[j], ln_out[0][j], ident_l)

            def cross_scores(p, j):
                pe.wait_ge(y1_cols_done[j], p + 1)
                pe.wait_ge(ctx_in[j], 32 * (p + 1))
                for hf in range(DH):
                    mm = pe.matmul(att_ps[j][0:L, 0:S], y1_cols[j][:, hf, :], ctx_cols[j][:, hf, :],
                                   start=(hf == 0), stop=(hf == DH - 1))
                mm.then_inc(cross_scored[j], 1)

            def cross_turn(p, j):
                pe.wait_ge(cross_exp[j], p + 1)
                for k in range(SK):
                    mm = pe.transpose(att_ps[j][0:SC, k * L:(k + 1) * L], cross_p[j][:, k * SC:(k + 1) * SC], ident_l)
                mm.then_inc(cross_turned[j], 1)

            def cross_mix(p, j):
                pe.wait_ge(cross_pt_done[j], p + 1)
                for k in range(SK):
                    mm = pe.matmul(att_ps[j][0:L, 0:D], cross_pt[j][:, k, :], ctx_rows[j][:, k, :],
                                   start=(k == 0), stop=(k == SK - 1))
                mm.then_inc(cross_mixed[j], 1)

            def turn_y2(p, j):
                pe.wait_ge(ln_done[1][j], p + 1)
                turn(att_ps[j], L, D, y2_turned[j], ln_out[1][j], ident_l)

            def feed_forward_1(q, u):
                if u == 0:
                    for j in range(2):
                        pe.wait_ge(y2_cols_done[j], q + 1)
                if u >= 2:
                    pe.wait_ge(hidden_done, q * FC + 2 * (u - 1))
                for i in range(2):
                    c = 2 * u + i
                    for hf in range(DH):
                        mm = pe.matmul(ff1_ps[u % 2][:, i * 2 * L:(i + 1) * 2 * L], w1[:, hf, c * P:(c + 1) * P],
                                       y2_cols[:, hf, :, :].rearrange("p j t -> p (j t)"),
                                       start=(hf == 0), stop=(hf == DH - 1))
                mm.then_inc(ff1_done, 1)

            def feed_forward_2(q, j):
                pe.wait_ge(hidden_done, (q + 1) * FC)
                pe.wait_ge(wo_copied[j], q + 1)
                for c in range(FC):
                    mm = pe.matmul(ff2_ps[j][0:L, 0:D], hidden[:, c, j, :], w2[:, c, :],
                                   start=(c == 0), stop=(c == FC - 1))
                mm.then_inc(ff2_done[j], 1)

            def turn_x2(q, j):
                pe.wait_ge(x2_done[j], q + 1)
                turn(ff2_ps[j], L, D, x2_turned[j], fresh[j][:, 0, :], ident_l)

            def gates(q, j):
                pe.wait_ge(x2_cols_done[j], q + 1)
                pe.wait_ge(cell_done, 2 * q + j + 1)
                for g in range(GATES):
                    for m in range(DH):
                        o = gate_ps[g // 2][:, ((g % 2) * DH + m) * L:((g % 2) * DH + m + 1) * L]
                        for w, cols in enumerate((x2_cols[j], cell2)):
                            for hf in range(DH):
                                mm = pe.matmul(o, gate_w[:, hf, w, g, m * P:(m + 1) * P], cols[:, hf, :],
                                               start=(w == 0 and hf == 0), stop=(w == 1 and hf == DH - 1))
                mm.then_inc(gates_done, 1)

            def output_x(q, j):
                for hf in range(DH):
                    mm = pe.matmul(ff2_ps[j][0:L, 0:D], x2_cols[j][:, hf, :], gate_w[:, hf, 0, 3, :],
                                   start=(hf == 0), stop=(hf == DH - 1))
                mm.then_inc(wo_done[j], 1)

            def pair_step(p, q):
                def both(stage):
                    if p is not None:
                        for j in range(2):
                            stage(p, j)

                def feed(stage, *which):
                    if q is not None:
                        stage(q, *which)

                both(self_turn_x1)
                feed(feed_forward_1, 0)
                feed(feed_forward_1, 1)
                both(self_scores)
                feed(feed_forward_1, 2)
                both(self_turn)
                feed(feed_forward_1, 3)
                both(self_mix)
                feed(feed_forward_2, 0)
                feed(feed_forward_2, 1)
                both(turn_y1)
                both(cross_scores)
                feed(turn_x2, 0)
                feed(gates, 0)
                both(cross_turn)
                feed(output_x, 0)
                feed(turn_x2, 1)
                both(cross_mix)
                feed(gates, 1)
                feed(output_x, 1)
                both(turn_y2)

            pe.wait_ge(small_in, 32)
            pair_step(0, None)
            pe.wait_ge(w_in, 48)
            pe.wait_ge(u_halved, 2)
            with nc.tensor.Fori(1, PAIRS) as p:
                pair_step(p, p - 1)
            pair_step(None, PAIRS - 1)
            pe.wait_ge(cell_done, B + 1)
            pe.wait_ge(wo_copied[0], PAIRS + 1)
            for hf in range(DH):
                mm = pe.matmul(ff2_ps[0][0:L, 0:D], cell2[:, hf, :], gate_w[:, hf, 1, 3, :],
                               start=(hf == 0), stop=(hf == DH - 1))
            mm.then_inc(u_done, 1)

        @block.vector
        def _(dve):
            def self_softmax(p, j):
                dve.wait_ge(self_scored[j], p + 1)
                dve.scalar_tensor_tensor(out=self_s[j][:, :], in0=att_ps[j][0:L, 0:L], scalar=SCORE, in1=causal,
                                         op0=ALU.mult, op1=ALU.add).then_inc(self_masked[j], 1)
                dve.wait_ge(self_masked[j], p + 1)
                dve.reduce_max(row_max[0][j][:, :], self_s[j][:, :], mybir.AxisListType.X).then_inc(self_max[j], 1)
                dve.wait_ge(self_max[j], p + 1)
                dve.tensor_scalar(neg_max[0][j][:, :], row_max[0][j][:, :], -1.0, None, ALU.mult)\
                    .then_inc(self_neg[j], 1)

            def self_inverse(p, j):
                dve.wait_ge(self_exp[j], p + 1)
                dve.reciprocal(inv_sum[0][j][:, :], row_sum[0][j][:, :]).then_inc(self_inv[j], 1)

            def cross_largest(p, j):
                dve.wait_ge(cross_scored[j], p + 1)
                dve.reduce_max(row_max[1][j][:, :], att_ps[j][0:L, 0:S], mybir.AxisListType.X).then_inc(cross_max[j], 1)
                dve.wait_ge(cross_max[j], p + 1)
                dve.tensor_scalar(neg_max[1][j][:, :], row_max[1][j][:, :], -SCORE, None, ALU.mult)\
                    .then_inc(cross_neg[j], 1)

            def cross_inverse(p, j):
                dve.wait_ge(cross_exp[j], p + 1)
                dve.reciprocal(inv_sum[1][j][:, :], row_sum[1][j][:, :]).then_inc(cross_inv[j], 1)

            def attention_residual(i, p, j):
                dve.wait_ge((self_mixed, cross_mixed)[i][j], p + 1)
                dve.wait_ge((self_inv, cross_inv)[i][j], p + 1)
                if i == 0:
                    dve.wait_ge(x1_in[j], 16 * (p + 1))
                else:
                    dve.wait_ge(ln_done[0][j], p + 1)
                dve.scalar_tensor_tensor(out=ln_in[i][j][:, :], in0=att_ps[j][0:L, 0:D], scalar=inv_sum[i][j][:, :],
                                         in1=(x1_att[j], ln_out[0][j])[i][:, :], op0=ALU.mult, op1=ALU.add)\
                    .then_inc(ln_summed[i][j], 1)

            def feed_residual(q, j):
                dve.wait_ge(ff2_done[j], q + 1)
                dve.wait_ge(y2_bias_done[j], q + 1)
                dve.tensor_tensor(ln_in[2][j][:, :], ff2_ps[j][0:L, 0:D], y2_bias[j][:, :], ALU.add)\
                    .then_inc(ln_summed[2][j], 1)

            def statistics(i, p, js):
                for j in js:
                    dve.wait_ge(ln_summed[i][j], p + 1)
                    dve.bn_stats(ln_stats[i][j][:, :], ln_in[i][j][:, :]).then_inc(ln_stat[i][j], 1)
                for j in js:
                    dve.wait_ge(ln_stat[i][j], p + 1)
                dve.memset(spare[:, :], 0.0)
                for j in js:
                    dve.bn_aggr(ln_mv[i][j][:, :], ln_stats[i][j][:, :]).then_inc(ln_agg[i][j], 1)
                for j in js:
                    dve.wait_ge(ln_agg[i][j], p + 1)
                    dve.tensor_scalar(ln_var[i][j][:, :], ln_mv[i][j][:, 1:2], EPS, None, ALU.add)\
                        .then_inc(ln_vared[i][j], 1)
                if i < 3:
                    for j in js:
                        centre(i, p, j)

            def centre(i, p, j):
                dve.scalar_tensor_tensor(out=ln_in[i][j][:, :], in0=ln_in[i][j][:, :], scalar=ln_mv[i][j][:, 0:1],
                                         in1=norm_w[:, 2 * i, :], op0=ALU.subtract, op1=ALU.mult)\
                    .then_inc(ln_centred[i][j], 1)

            def normalise(i, p, j):
                dve.wait_ge(ln_centred[i][j], p + 1)
                dve.wait_ge(ln_rooted[i][j], p + 1)
                dve.scalar_tensor_tensor(out=ln_out[i][j][:, :], in0=ln_in[i][j][:, :], scalar=ln_rstd[i][j][:, :],
                                         in1=norm_w[:, 2 * i + 1, :], op0=ALU.mult, op1=ALU.add)\
                    .then_inc(ln_done[i][j], 1)

            def outer_residual(q, j):
                dve.wait_ge(ln_centred[2][j], q + 1)
                dve.wait_ge(ln_rooted[2][j], q + 1)
                dve.wait_ge(x1_beta_done[j], q + 1)
                dve.scalar_tensor_tensor(out=ln_in[3][j][:, :], in0=ln_in[2][j][:, :], scalar=ln_rstd[2][j][:, :],
                                         in1=x1_res[j][:, :], op0=ALU.mult, op1=ALU.add)\
                    .then_inc(ln_summed[3][j], 1)

            def normalise_x2(q, j):
                dve.wait_ge(ln_rooted[3][j], q + 1)
                dve.wait_ge(rows_kept[j], 16 * (q + 1))
                dve.tensor_scalar(fresh[j][:, 0, :], ln_in[3][j][:, :], ln_mv[3][j][:, 0:1], ln_rstd[3][j][:, :],
                                  ALU.subtract, ALU.mult).then_inc(x2_done[j], 1)

            def cell(q, j):
                n = 2 * q + j + 1
                dve.wait_ge(gates_tanh, GATES * DH * n)
                dve.scalar_tensor_tensor(out=kept[:, :, :], in0=gate_t[:, 0, :, :], scalar=1.0, in1=cell2[:, :, :],
                                         op0=ALU.add, op1=ALU.mult).then_inc(cell_kept, 1)
                dve.scalar_tensor_tensor(out=added[:, :, :], in0=gate_t[:, 1, :, :], scalar=1.0, in1=gate_t[:, 2, :, :],
                                         op0=ALU.add, op1=ALU.mult).then_inc(cell_added, 1)
                dve.wait_ge(cell_kept, n)
                dve.wait_ge(cell_added, n)
                dve.scalar_tensor_tensor(out=cell2[:, :, :], in0=kept[:, :, :], scalar=0.5, in1=added[:, :, :],
                                         op0=ALU.mult, op1=ALU.add).then_inc(cell_done, 1)

            def pair_step(p, q):
                if p is not None:
                    for j in range(2):
                        self_softmax(p, j)
                    for j in range(2):
                        self_inverse(p, j)
                    for j in range(2):
                        attention_residual(0, p, j)
                    statistics(0, p, (0, 1))
                    for j in range(2):
                        normalise(0, p, j)
                if q is not None:
                    feed_residual(q, 0)
                    statistics(2, q, (0,))
                    outer_residual(q, 0)
                    statistics(3, q, (0,))
                    feed_residual(q, 1)
                    normalise_x2(q, 0)
                    statistics(2, q, (1,))
                if p is not None:
                    for j in range(2):
                        cross_largest(p, j)
                if q is not None:
                    outer_residual(q, 1)
                    statistics(3, q, (1,))
                    normalise_x2(q, 1)
                if p is not None:
                    for j in range(2):
                        cross_inverse(p, j)
                if q is not None:
                    cell(q, 0)
                if p is not None:
                    for j in range(2):
                        attention_residual(1, p, j)
                    statistics(1, p, (0, 1))
                    for j in range(2):
                        normalise(1, p, j)
                if q is not None:
                    cell(q, 1)

            for j in range(2):
                dve.sem_inc(rows_kept[j], 16)
            dve.memset(ones_l[:, :], 1.0).then_inc(ones_done, 1)
            dve.wait_ge(small_in, 32)
            dve.tensor_scalar(gate_b[:, 0:2, :], gate_b[:, 0:2, :], 0.5, None, ALU.mult).then_inc(gate_b_halved, 1)
            dve.wait_ge(ones_done, 1)
            for hf in range(DH):
                ins = dve.tensor_scalar(cell2[:, hf, :], ones_l[:, :], in_c[:, hf:hf + 1], 2.0, ALU.mult, ALU.mult)
            ins.then_inc(cell_done, 1)
            dve.wait_ge(n_in, 128)
            pair_step(0, None)
            dve.wait_ge(w_in, 48)
            for hf in range(DH):
                u = gate_w[:, hf, 1, :, :]
                dve.tensor_scalar(u, u, 0.5, None, ALU.mult).then_inc(u_halved, 1)
            with nc.vector.Fori(1, PAIRS) as p:
                pair_step(p, p - 1)
            pair_step(None, PAIRS - 1)
            dve.wait_ge(u_done, 1)
            dve.wait_ge(n_in, 128)
            dve.tensor_tensor(base[:, :], ff2_ps[0][0:L, 0:D], norm_w[:, 7, :], ALU.add).then_inc(base_done, 1)
            dve.wait_ge(base_done, 1)
            for j in range(2):
                dve.wait_ge(rows_kept[j], 16 * (PAIRS + 1))
            for q in range(B // GROUP):
                t = wo_all[:, q * GROUP:(q + 1) * GROUP, :]
                dve.tensor_tensor(t, t, base[:, :].unsqueeze(1).broadcast_to([L, GROUP, D]), ALU.add)\
                    .then_inc(fin_arg, 1)

            def finish(q):
                r = range(q * GROUP, (q + 1) * GROUP)
                x = x2_all[:, r.start:r.stop, :]
                dve.wait_ge(fin_tanh, q + 1)
                dve.tensor_tensor(x, x, wo_all[:, r.start:r.stop, :], ALU.add).then_inc(fin_sum, 1)
                dve.wait_ge(fin_sum, q + 1)
                for b in r:
                    dve.bn_stats(fin_stats[:, b, :], x2_all[:, b, :]).then_inc(fin_stat, 1)
                dve.wait_ge(fin_stat, r.stop)
                for b in r:
                    dve.bn_aggr(fin_mv[:, b, :], fin_stats[:, b, :]).then_inc(fin_agg, 1)
                dve.wait_ge(fin_agg, r.stop)
                dve.tensor_scalar(fin_var[:, r.start:r.stop], fin_mv[:, r.start:r.stop, 1], EPS, None, ALU.add)\
                    .then_inc(fin_vared, 1)

            def finish_rows(q):
                dve.wait_ge(fin_rooted, q + 1)
                for b in range(q * GROUP, (q + 1) * GROUP):
                    dve.tensor_scalar(x2_all[:, b, :], x2_all[:, b, :], fin_mv[:, b, 0:1], fin_rstd[:, b:b + 1],
                                      ALU.subtract, ALU.mult).then_inc(fin_normed, 1)

            for q in range(B // GROUP):
                finish(q)
                if q:
                    finish_rows(q - 1)
            finish_rows(B // GROUP - 1)


_DIRECT = ['x', 'ctx_1024', 'L0_attn_bdt', 'L0_attn_A_log', 'L0_attn_Dp', 'L0_xattn_w1', 'L0_xattn_w2',
           'L0_xattn_b2', 'L0_xattn_g1', 'L0_xattn_beta1', 'L0_xattn_g2', 'L0_xattn_beta2', 'L0_xattn_g3',
           'L0_xattn_beta3', 'L0_ffn_bo']


def build(nc, args, out):
    x1 = nc.dram_tensor("x1", (B, L, D), F32, kind="Internal").ap()
    used = []
    state_space(nc, used, args, x1)
    nc.clear_and_free_semaphores(used)
    nc.all_engine_barrier()
    decoder_and_cell(nc, [], args, x1, out)


def kernel(**inputs):
    import numpy as _np
    import concourse.bacc as _bacc
    from concourse import mybir as _mybir
    from concourse.bass_utils import run_bass_kernel_spmd as _run

    def turned(names):
        return _np.ascontiguousarray(_np.concatenate([_np.asarray(inputs[n]).T for n in names], axis=1))

    nc = _bacc.Bacc("TRN2", target_bir_lowering=False, num_devices=1)
    laid = {name: _np.ascontiguousarray(inputs[name]) for name in _DIRECT}
    laid["xT"] = _np.ascontiguousarray(_np.asarray(inputs["x"]).reshape(TOK, D).T)
    laid["ctxT"] = _np.ascontiguousarray(_np.asarray(inputs["ctx_1024"]).transpose(0, 2, 1))
    laid["projT"] = turned(["L0_attn_Wdt", "L0_attn_WB", "L0_attn_WC"])
    laid["gateT"] = turned([f"L0_ffn_{w}{g}" for w in "wu" for g in "fico"])
    laid["vectors"] = _np.ascontiguousarray(_np.concatenate(
        [_np.asarray(inputs[n]).reshape(-1, P) for n in
         ("L0_xattn_b1", "L0_ffn_bf", "L0_ffn_bi", "L0_ffn_bc", "L0_ffn_in_c")], axis=0).T)
    laid["consts"] = shape_constants()
    args = {n: nc.dram_tensor(f"in_{n}", a.shape, _mybir.dt.from_np(a.dtype), kind="ExternalInput").ap()
            for n, a in laid.items()}
    out = nc.dram_tensor("out_0", (B, L, D), F32, kind="ExternalOutput").ap()
    build(nc, args, out)
    r = _run(nc, [{f"in_{n}": a for n, a in laid.items()}], core_ids=[0])
    return r.results[0]["out_0"]
```

```python
from contextlib import ExitStack

import numpy as np

import concourse.bass as bass
from concourse import mybir

F32 = mybir.dt.float32
BF16 = mybir.dt.bfloat16
ALU = mybir.AluOpType
ACT = mybir.ActivationFunctionType
P = 128

B, L, D, N = 16, 112, 256, 16
TOK = B * L
TILES = TOK // P
DH = D // P
HT = TILES // 2
CH = 2
CB = B // CH
TB = 16
BLOCKS = L // TB
AHEAD = 8
LEAD = 4
ACT_WIDENS = 2
EARLY = 4
EPS = 1e-5
CLAMP = 20.0
DT_C, DT_R = (0.1 + 0.001) / 2.0, (0.1 - 0.001) / 2.0
V_PIECES = (3, 3, 2)
COMBOS = sum(V_PIECES)


def shape_constants():
    p = np.arange(P)
    ident = np.eye(P, dtype=np.float32)
    block_ones = (p[:, None] // N == p[None, :] // N).astype(np.float32)
    own_batch = (p[:, None] // N == np.arange(CB)[None, :]).astype(np.float32)
    row_batch = (p[:, None] % B == np.arange(B)[None, :]).astype(np.float32)
    causal = np.where(p[:, None] >= np.arange(L)[None, :], 0.0, -1e30).astype(np.float32)
    return np.ascontiguousarray(np.concatenate([ident, block_ones, own_batch, row_batch, causal], axis=1))


def state_space(nc, used, a, x1):
    with ExitStack() as ctx:
        def sb(name, shape, dt=F32):
            return ctx.enter_context(nc.sbuf_tensor(name, shape, dt))

        def pb(name, shape, dt=F32):
            return ctx.enter_context(nc.psum_tensor(name, shape, dt))

        def sem(name):
            used.append(nc.alloc_semaphore(name))
            return used[-1]

        v_scratch = nc.dram_tensor("v_pieces", (3, TOK, D), BF16, kind="Internal").ap()
        b_scratch = nc.dram_tensor("b_pieces", (3, TOK, N), BF16, kind="Internal").ap()
        c_scratch = nc.dram_tensor("c_param", (N, TOK), F32, kind="Internal").ap()

        const = sb("const", [P, a["consts"].shape[1]])
        ident = const[:, 0:P]
        block_ones = const[:, P:2 * P]
        own_batch = const[:, 2 * P:2 * P + CB]
        row_batch = const[:, 2 * P + CB:2 * P + CB + B]
        turned_c = sb("turned_c", [P, CH * TB * (P + CB)])
        x_rows = turned_c[:, 0:TILES * D]
        x_cols = sb("x_cols", [P, DH * TOK])
        v_hi = x_cols[:, 0:TILES * D // 2].bitcast(BF16)
        v_mid = x_cols[:, TILES * D // 2:TILES * D].bitcast(BF16)
        proj_w = sb("proj_w", [P, DH, D + 2 * N])
        a_exp = sb("a_exp", [P, DH, N])
        bdt = sb("bdt", [P, D])
        dp1 = sb("dp1", [P, D])
        tanh_bias = sb("tanh_bias", [P, 1])
        dt_cols = sb("dt_cols", [P, DH, TOK + AHEAD])
        c_col = sb("c_col", [P, CH, L])
        b_rows = sb("b_rows", [P, L * N], BF16)
        v_rows = sb("v_rows", [P, (L + 1) * D], BF16)
        c_rows = v_rows[0:N, 0:2 * TOK].bitcast(F32)
        v_lo = v_rows[:, 2 * TOK:2 * TOK + TILES * D]
        b_wide = [sb(f"b_wide{c}", [P, (L + 1) * P], BF16) for c in range(CH)]
        bn = TILES * N
        bc = b_wide[1][:, 0:2 * bn].bitcast(F32)
        b_work = b_wide[1][:, 2 * bn:4 * bn].bitcast(F32)
        b_pc = b_wide[1][:, 4 * bn:7 * bn].rearrange("p (q n) -> p q n", q=3)
        ring = sb("ring", [P, TB, DH, CH, CB * N])
        flat = ring[:, :, :, :, :].rearrange("p t h c n -> p (t h c n)")
        dt_rows = flat[:, 0:TILES * D]
        v_work = flat[:, TILES * D:2 * TILES * D]
        rows = [x_cols[:, i * D:(i + 1) * D] for i in range(DH * TOK // D)]
        turned_set = [turned_c[:, c * TB * (P + CB):(c + 1) * TB * (P + CB)] for c in range(CH)]
        turned_diagonal = [t.rearrange("p (t m) -> p t m", m=P + CB)[:, :, 0:CB] for t in turned_set]
        h = [rows[2 * c:2 * c + 2] for c in range(CH)]
        squares, x_blk, x_skip, res, normed = (rows[i:i + 2] for i in range(4, 14, 2))
        decayed = [sb(f"decayed{c}", [P, D]) for c in range(CH)]
        sumsq = [sb(f"sumsq{c}", [P, 1]) for c in range(CH)]
        clamped = [sb(f"clamped{c}", [P, 1]) for c in range(CH)]
        scale = [sb(f"scale{c}", [P, TB]) for c in range(CH)]
        own_scale = [sb(f"own_scale{c}", [P, TB, CB]) for c in range(CH)]
        row_scale = [sb(f"row_scale{c}", [P, 1]) for c in range(CH)]
        sixteenth = sb("sixteenth", [P, 1])
        minus_half = sb("minus_half", [P, 1])
        y_rows = [sb(f"y_rows{c}", [P, D]) for c in range(CH)]
        stats = [sb(f"stats{c}", [P, 6]) for c in range(CH)]
        moments = [sb(f"moments{c}", [P, 2]) for c in range(CH)]
        var_eps = [sb(f"var_eps{c}", [P, 1]) for c in range(CH)]
        rstd = [sb(f"rstd{c}", [P, 1]) for c in range(CH)]

        decay_ps = [pb(f"decay_ps{c}", [P, 2 * D]) for c in range(CH)]
        input_ps = [pb(f"input_ps{c}", [P, 2 * D]) for c in range(CH)]
        y_ps = [pb(f"y_ps{c}", [P, 2 * D]) for c in range(CH)]
        norm_ps = [pb(f"norm_ps{c}", [P, 2 * D]) for c in range(CH)]
        proj_ps = [decay_ps[0], decay_ps[1], input_ps[0], input_ps[1]]

        consts_in = sem("consts_in")
        x_cols_in = [sem(f"x_cols_in{i}") for i in range(2)]
        x_rows_in = sem("x_rows_in")
        projected = sem("projected")
        c_projected = sem("c_projected")
        bias_added = sem("bias_added")
        c_copied = sem("c_copied")
        b_split = sem("b_split")
        b_stored = sem("b_stored")
        c_stored = sem("c_stored")
        b_loaded = sem("b_loaded")
        c_loaded = sem("c_loaded")
        b_widened = sem("b_widened")
        negated = sem("negated")
        softplus_ln = sem("softplus_ln")
        act_chain = sem("act_chain")
        dt_tanh = sem("dt_tanh")
        dt_done = sem("dt_done")
        dt_turned = sem("dt_turned")
        dt_cols_done = sem("dt_cols_done")
        dt_scaled = sem("dt_scaled")
        v_made = sem("v_made")
        v_hi_done, v_rest_done, v_mid_done, v_lo_done = sem("v_hi_done"), sem("v_rest_done"), sem("v_mid_done"), sem("v_lo_done")
        v_stored = sem("v_stored")
        v_early, v_loaded = sem("v_early"), sem("v_loaded")
        a_ready = sem("a_ready")
        pad_zeroed = sem("pad_zeroed")
        zeroed = sem("zeroed")
        dve_chain = sem("dve_chain")
        pool_chain = sem("pool_chain")
        z_low = sem("z_low")
        z_high = sem("z_high")
        c_spread = [sem(f"c_spread{c}") for c in range(CH)]
        x_skip_free = [sem(f"x_skip_free{c}") for c in range(CH)]
        tanh_done = sem("tanh_done")
        decay_done = sem("decay_done")
        decay_turned = [sem(f"decay_turned{c}") for c in range(CH)]
        input_done = [sem(f"input_done{c}") for c in range(CH)]
        h_done = [sem(f"h_done{c}") for c in range(CH)]
        decayed_done = [sem(f"decayed_done{c}") for c in range(CH)]
        squared = [sem(f"squared{c}") for c in range(CH)]
        normsq_done = [sem(f"normsq_done{c}") for c in range(CH)]
        clamped_done = [sem(f"clamped_done{c}") for c in range(CH)]
        scale_done = [sem(f"scale_done{c}") for c in range(CH)]
        scale_spread = [sem(f"scale_spread{c}") for c in range(CH)]
        rowscale_done = [sem(f"rowscale_done{c}") for c in range(CH)]
        rowscale_copied = [sem(f"rowscale_copied{c}") for c in range(CH)]
        y_step = [sem(f"y_step{c}") for c in range(CH)]
        y_taken = [sem(f"y_taken{c}") for c in range(CH)]
        xblk_in = [sem(f"xblk_in{c}") for c in range(CH)]
        xskip_done = [sem(f"xskip_done{c}") for c in range(CH)]
        stats_done = [sem(f"stats_done{c}") for c in range(CH)]
        moments_done = [sem(f"moments_done{c}") for c in range(CH)]
        var_done = [sem(f"var_done{c}") for c in range(CH)]
        rstd_done = [sem(f"rstd_done{c}") for c in range(CH)]
        normed_done = [sem(f"normed_done{c}") for c in range(CH)]
        x1_stored = [sem(f"x1_stored{c}") for c in range(CH)]

        def half(t, i):
            return t[:, i * HT * D:(i + 1) * HT * D]


        def widening(b, part):
            wide = b_wide[b // CB][:, part * L // 2 * P:(part + 1) * L // 2 * P]
            return (wide.rearrange("p (t b n) -> p t b n", b=CB, n=N)[:, :, b % CB, :],
                    b_rows[:, part * L // 2 * N:(part + 1) * L // 2 * N].rearrange("p (t n) -> p t n", n=N),
                    row_batch[:, b:b + 1])

        block = ctx.enter_context(nc.Block())

        @block.sync
        def _(sp):
            sp.dma_start(const[:, :], a["consts"]).then_inc(consts_in, 16)
            sp.dma_start(proj_w[:, :, :], a["projT"].rearrange("(h p) n -> p h n", p=P)).then_inc(consts_in, 16)
            sp.dma_start(bdt[:, :], a["L0_attn_bdt"].unsqueeze(0).broadcast_to([P, D])).then_inc(consts_in, 16)
            sp.dma_start(a_exp[:, :, :], a["L0_attn_A_log"].rearrange("(h p) n -> p h n", p=P)).then_inc(consts_in, 16)
            sp.dma_start(dp1[:, :], a["L0_attn_Dp"].unsqueeze(0).broadcast_to([P, D])).then_inc(consts_in, 16)
            for i in range(2):
                sp.dma_start(x_cols[:, :].rearrange("p (h n) -> p h n", h=DH)[:, :, i * HT * P:(i + 1) * HT * P],
                             a["xT"].rearrange("(h p) n -> p h n", p=P)[:, :, i * HT * P:(i + 1) * HT * P])\
                    .then_inc(x_cols_in[i], 16)
            sp.dma_start(x_rows.rearrange("p (j d) -> p j d", j=TILES),
                         a["x"].rearrange("b t d -> (b t) d").rearrange("(j p) d -> p j d", p=P)).then_inc(x_rows_in, 16)
            sp.wait_ge(b_split, 3)
            for q in range(3):
                sp.dma_start(b_scratch[q].rearrange("(j p) n -> p j n", p=P),
                             b_pc[:, q, :].rearrange("p (j n) -> p j n", j=TILES)).then_inc(b_stored, 16)
            sp.wait_ge(b_stored, 48)
            for q, count in enumerate(V_PIECES):
                sp.dma_start(b_rows[3 * q * B:(3 * q + count) * B, :],
                             b_scratch[q].rearrange("(b t) n -> b (t n)", b=B).unsqueeze(0)
                             .broadcast_to([count, B, L * N])).then_inc(b_loaded, 16)
            for q, (piece, done) in enumerate(((v_hi, v_hi_done), (v_mid, v_mid_done), (v_lo, v_lo_done))):
                for i in range(2):
                    sp.wait_ge(done, i + 1)
                    sp.dma_start(v_scratch[q, i * HT * P:(i + 1) * HT * P].rearrange("(j p) d -> p j d", p=P),
                                 half(piece, i).rearrange("p (j d) -> p j d", j=HT)).then_inc(v_stored, 16)
                if q == 0:
                    sp.wait_ge(c_copied, 4)
                    sp.dma_start(c_scratch, c_rows).then_inc(c_stored, 16)
                if q == 2:
                    sp.wait_ge(c_stored, 16)
                    for c in range(CH):
                        sp.dma_start(c_col[:, c, :], c_scratch.rearrange("n (b t) -> b n t", b=B)
                                     [c * CB:(c + 1) * CB]).then_inc(c_loaded, 16)
            sp.wait_ge(v_stored, 96)

            def load_v(start, size, at, done=v_loaded):
                for q, count in enumerate(V_PIECES):
                    sp.dma_start(v_rows[3 * q * B:(3 * q + count) * B, bass.ds(at * D, size * D)],
                                 v_scratch[0:count].rearrange("q (b t) d -> (q b) (t d)", b=B)
                                 [:, bass.ds(start * D, size * D)]).then_inc(done, 16)

            load_v(0, EARLY, 0, v_early)
            load_v(EARLY, TB - EARLY, EARLY)
            for c in range(CH):
                sp.sem_inc(x1_stored[c], 16)

            def rows_of(dram, k, c):
                return dram[c * CB:(c + 1) * CB, bass.ds(k * TB, TB), :].rearrange("b t d -> t b d")

            def load_x_rows(k):
                for c in range(CH):
                    sp.wait_ge(xskip_done[c], k + 1)
                    sp.dma_start(x_blk[c], rows_of(a["x"], k, c))\
                        .then_inc(xblk_in[c], 16)

            def store_x1_rows(k):
                for c in range(CH):
                    sp.wait_ge(normed_done[c], k + 1)
                    sp.dma_start(rows_of(x1, k, c), normed[c])\
                        .then_inc(x1_stored[c], 16)

            def load_next_v(k):
                sp.wait_ge(v_loaded, 16 * len(V_PIECES) * (k + 1))
                load_v((k + 1) * TB, TB, (k + 1) * TB)

            load_x_rows(0)
            load_next_v(0)
            with nc.sync.Fori(1, BLOCKS - 1) as k:
                load_x_rows(k)
                load_next_v(k)
                store_x1_rows(k - 1)
            load_x_rows(BLOCKS - 1)
            sp.wait_ge(v_loaded, 16 * len(V_PIECES) * BLOCKS)
            load_v(0, 1, L)
            store_x1_rows(BLOCKS - 2)
            store_x1_rows(BLOCKS - 1)
            for c in range(CH):
                sp.wait_ge(x1_stored[c], 16 * BLOCKS + 16)

        @block.gpsimd
        def _(g):
            g.memset(minus_half[:, :], -0.5).then_inc(pool_chain, 1)
            g.memset(sixteenth[:, :], 1.0 / N).then_inc(pool_chain, 1)
            g.wait_ge(pool_chain, 2)
            for c in range(CH):
                g.sem_inc(xskip_done[c], 1)
                g.sem_inc(scale_done[c], 1)
                g.sem_inc(x_skip_free[c], 1)
            g.wait_ge(consts_in, 80)
            g.tensor_scalar(dp1[:, :], dp1[:, :], 1.0, None, ALU.add).then_inc(pool_chain, 1)
            g.wait_ge(pool_chain, 3)

            def half_of_decay_arguments(T, slot, c):
                g.wait_ge(decay_turned[c], T + 1)
                dt_col = dt_cols[:, 0, bass.ds(c * (CB * L) + T, CB, step=L)]
                g.tensor_tensor(ring[:, slot, 0, c, :].rearrange("p (b n) -> p b n", n=N),
                                dt_col.unsqueeze(2).broadcast_to([P, CB, N]),
                                a_exp[:, 0, :].unsqueeze(1).broadcast_to([P, CB, N]),
                                ALU.mult).then_inc(z_low, 1)

            def inverse_norm(T, s, c):
                g.wait_ge(clamped_done[c], T + 1)
                g.tensor_tensor(scale[c][:, s:s + 1], clamped[c][:, :], minus_half[:, :], ALU.pow)\
                    .then_inc(scale_done[c], 1)

            def spread_scales(k):
                for c in range(CH):
                    g.wait_ge(scale_done[c], k * TB + 1)
                    g.tensor_tensor(own_scale[c][:, :, :], scale[c][:, :].unsqueeze(2).broadcast_to([P, TB, CB]),
                                    own_batch.unsqueeze(1).broadcast_to([P, TB, CB]), ALU.mult)\
                        .then_inc(scale_spread[c], 1)

            def spread_c(k, c):
                g.wait_ge(y_step[c], k * TB + 2)
                g.tensor_tensor(turned_diagonal[c], c_col[:, c, bass.ds(k * TB, TB)].unsqueeze(2).broadcast_to([P, TB, CB]),
                                own_batch.unsqueeze(1).broadcast_to([P, TB, CB]), ALU.mult).then_inc(c_spread[c], 1)

            def block_steps(k, first):
                for s in range(TB):
                    T = k * TB + s
                    if s or not first:
                        inverse_norm(T - 1, (s - 1) % TB, 1)
                    if s == 0:
                        if not first:
                            spread_scales(k)
                            g.wait_ge(scale_spread[0], k)
                            g.wait_ge(scale_spread[1], k)
                        inverse_norm(T, s, 0)
                        if not first:
                            for c in range(CH):
                                spread_c(k, c)
                        half_of_decay_arguments(T + AHEAD, (s + AHEAD) % TB, 0)
                        continue
                    if s == 1:
                        half_of_decay_arguments(T - 1 + AHEAD, (s - 1 + AHEAD) % TB, 1)
                    half_of_decay_arguments(T + AHEAD, (s + AHEAD) % TB, 0)
                    inverse_norm(T, s, 0)
                    half_of_decay_arguments(T + AHEAD, (s + AHEAD) % TB, 1)
                    if s in (4, 5, 6, 7):
                        c, part = (s - 4) // 2, slice(s % 2 * P, (s % 2 + 1) * P)
                        if s % 2 == 0:
                            g.wait_ge(xblk_in[c], 16 * (k + 1))
                            g.wait_ge(x_skip_free[c], k + 1)
                        ins = g.tensor_tensor(x_skip[c][:, part], x_blk[c][:, part], dp1[:, part], ALU.mult)
                        if s % 2:
                            ins.then_inc(xskip_done[c], 1)
                    if s in (10, 11) and not first:
                        inverse_deviation(k, s - 10)

            def inverse_deviation(k, c):
                g.wait_ge(var_done[c], k)
                g.tensor_tensor(rstd[c][:, :], var_eps[c][:, :], minus_half[:, :], ALU.pow).then_inc(rstd_done[c], 1)

            g.wait_ge(v_made, 2)
            g.memset(turned_c[:, :], 0.0).then_inc(pool_chain, 1)
            g.wait_ge(a_ready, 2)
            g.wait_ge(dt_cols_done, TILES)
            g.wait_ge(pad_zeroed, 1)
            for T in range(AHEAD):
                if T == AHEAD - 1:
                    g.wait_ge(v_lo_done, 2)
                for c in range(CH):
                    half_of_decay_arguments(T, T, c)
            g.wait_ge(pool_chain, 4)
            g.wait_ge(c_loaded, 32)
            for c in range(CH):
                spread_c(0, c)
            block_steps(0, True)
            with nc.gpsimd.Fori(1, BLOCKS) as k:
                block_steps(k, False)
            inverse_norm(L - 1, TB - 1, 1)
            spread_scales(BLOCKS)
            for c in range(CH):
                inverse_deviation(BLOCKS, c)

        @block.scalar
        def _(act):
            for i in range(2):
                act.wait_ge(negated, (i + 1) * HT)
                act.activation(half(v_work, i), half(v_work, i), ACT.Exp).then_inc(act_chain, 1)
            for i in range(2):
                act.wait_ge(act_chain, i + 1)
                act.activation(half(v_work, i), half(v_work, i), ACT.Ln, bias=1.0).then_inc(softplus_ln, 1)
            act.wait_ge(consts_in, 80)
            act.activation(a_exp[:, :, :], a_exp[:, :, :], ACT.Tanh, scale=0.5 / (5.0 + 1e-8)).then_inc(a_ready, 1)
            act.wait_ge(a_ready, 1)
            act.activation(a_exp[:, :, :], a_exp[:, :, :], ACT.Exp, scale=10.0).then_inc(a_ready, 1)
            for i in range(2):
                act.wait_ge(dt_done, i + 1)
                act.activation(half(dt_rows, i), half(dt_rows, i), ACT.Tanh, bias=tanh_bias[:, :],
                               scale=0.5 / (DT_R + 1e-8)).then_inc(dt_tanh, 1)
            act.wait_ge(c_projected, 4)
            def high_piece(i):
                act.wait_ge(v_made, i + 1)
                act.activation(half(v_hi, i), half(v_work, i), ACT.Copy).then_inc(v_hi_done, 1)

            def middle_piece(i):
                act.wait_ge(v_rest_done, i + 1)
                act.activation(half(v_mid, i), half(v_work, i), ACT.Copy).then_inc(v_mid_done, 1)

            def dt_columns(i):
                for j in range(i * HT, (i + 1) * HT):
                    act.wait_ge(dt_turned, j + 1)
                    act.activation(dt_cols[:, :, j * P:(j + 1) * P],
                                   proj_ps[j % 4][:, 0:DH * P].rearrange("p (h n) -> p h n", h=DH), ACT.Copy)\
                        .then_inc(dt_cols_done, 1)

            high_piece(0)
            dt_columns(0)
            high_piece(1)
            middle_piece(0)
            middle_piece(1)
            dt_columns(1)

            def decay_tanh(T, slot):
                act.wait_ge(z_low, (T + 1) * CH)
                act.wait_ge(z_high, T + 1)
                act.activation(ring[:, slot], ring[:, slot], ACT.Tanh, scale=-0.5 / (8.0 + 1e-8)).then_inc(tanh_done, 1)

            def decay_exp(T, slot):
                act.wait_ge(tanh_done, T + 1)
                act.activation(ring[:, slot], ring[:, slot], ACT.Exp, scale=16.0).then_inc(decay_done, 1)

            def square(T, s, c):
                act.wait_ge(h_done[c], T + 1)
                act.activation(squares[c], h[c][s % 2], ACT.Square, scale=1.0 / CLAMP,
                               accum_out=sumsq[c][:, :]).then_inc(squared[c], 1)

            for T in range(LEAD):
                decay_tanh(T, T)
                decay_exp(T, T)

            def take_outputs(k, c):
                act.wait_ge(y_step[c], k * TB + TB + 2)
                act.wait_ge(x_skip_free[c], k + 1)
                act.activation(y_rows[c][:, :], y_ps[c][:, 0:D], ACT.Copy).then_inc(y_taken[c], 1)

            def block_steps(k, first):
                for s in range(TB):
                    T = k * TB + s
                    square(T, s, 0)
                    if s == 0 and not first:
                        take_outputs(k - 1, 0)
                    decay_tanh(T + LEAD, (s + LEAD) % TB)
                    square(T, s, 1)
                    if s == 0 and not first:
                        take_outputs(k - 1, 1)
                    decay_exp(T + LEAD, (s + LEAD) % TB)

            act.wait_ge(b_loaded, 16 * len(V_PIECES))
            for b in range(B - ACT_WIDENS, B):
                wide, b_all, own = widening(b, 0)
                act.activation(wide, b_all, ACT.Identity, scale=own).then_inc(b_widened, 1)
            for c in range(CH):
                act.sem_inc(y_taken[c], 1)
            block_steps(0, True)
            with nc.scalar.Fori(1, BLOCKS) as k:
                block_steps(k, False)
            for c in range(CH):
                take_outputs(BLOCKS - 1, c)

        @block.tensor
        def _(pe):
            pe.wait_ge(consts_in, 80)
            xc = x_cols[:, :].rearrange("p (h n) -> p h n", h=DH)
            for j in range(TILES):
                if j % HT == 0:
                    pe.wait_ge(x_cols_in[j // HT], 16)
                if j >= 4:
                    pe.wait_ge(bias_added, j - 3)
                for hf in range(DH):
                    mm = pe.matmul(proj_ps[j % 4][:, 0:D + N], xc[:, hf, j * P:(j + 1) * P],
                                   proj_w[:, hf, 0:D + N], start=(hf == 0), stop=(hf == DH - 1))
                mm.then_inc(projected, 1)
            q = TOK // 4
            for j in range(4):
                for hf in range(DH):
                    mm = pe.matmul((y_ps + norm_ps)[j][0:N, 0:q], proj_w[:, hf, D + N:D + 2 * N],
                                   xc[:, hf, j * q:(j + 1) * q], start=(hf == 0), stop=(hf == DH - 1))
                mm.then_inc(c_projected, 1)
            pe.wait_ge(bias_added, TILES)
            for j in range(TILES):
                if j % HT == 0:
                    pe.wait_ge(dt_scaled, j // HT + 1)
                if j >= 4:
                    pe.wait_ge(dt_cols_done, j - 3)
                for hf in range(DH):
                    mm = pe.transpose(proj_ps[j % 4][:, hf * P:(hf + 1) * P],
                                      dt_rows[:, j * D + hf * P:j * D + (hf + 1) * P], ident)
                mm.then_inc(dt_turned, 1)
            for c in range(CH):
                pe.sem_inc(decay_turned[c], 1 + AHEAD)
                pe.sem_inc(y_step[c], 2)

            def turn_decay(T, s, c):
                pe.wait_ge(decay_done, T + 1)
                for hf in range(DH):
                    mm = pe.transpose(decay_ps[c][:, hf * P:(hf + 1) * P],
                                      ring[:, s % TB, hf, c, :], ident)
                mm.then_inc(decay_turned[c], 1)

            def input_product(T, s, c):
                pe.matmul(input_ps[c][:, 0:D], b_wide[c][:, bass.ds(T * P, P)],
                          v_rows[:, bass.ds(T * D, D)], start=True, stop=True).then_inc(input_done[c], 1)

            def norm_product(T, c):
                pe.wait_ge(squared[c], T + 1)
                pe.matmul(norm_ps[c][:, 0:1], block_ones, sumsq[c][:, :], start=True, stop=True)\
                    .then_inc(normsq_done[c], 1)

            def output_product(T, k, s, c):
                if s == 0:
                    pe.wait_ge(y_taken[c], k + 1)
                    pe.wait_ge(c_spread[c], k + 1)
                pe.matmul(y_ps[c][:, 0:D], turned_set[c][:, s * P:(s + 1) * P],
                          h[c][s % 2], start=(s == 0), stop=(s == TB - 1)).then_inc(y_step[c], 1)

            def row_scale_product(k, c):
                pe.wait_ge(scale_spread[c], k)
                pe.matmul(decay_ps[c][:, D:D + 1], own_scale[c][:, :, :].rearrange("p t b -> p (t b)"),
                          sixteenth[:, :], start=True, stop=True).then_inc(rowscale_done[c], 1)

            def block_steps(k, first):
                for s in range(TB):
                    T = k * TB + s
                    if first and s == EARLY - 1:
                        pe.wait_ge(v_loaded, 16 * len(V_PIECES))
                    if s == TB - 1:
                        pe.wait_ge(v_loaded, 16 * len(V_PIECES) * (k + 2))
                    for c in range(CH):
                        if s:
                            output_product(T - 1, k, s - 1, c)
                        elif not first:
                            output_product(T - 1, k - 1, TB - 1, c)
                        pe.wait_ge(h_done[c], T + 1)
                        input_product(T + 1, s + 1, c)
                        norm_product(T, c)
                        pe.wait_ge(decayed_done[c], T + 3)
                        turn_decay(T + 2, s + 2, c)
                        if s == 1 and not first:
                            row_scale_product(k, c)

            pe.wait_ge(dt_cols_done, TILES)
            pe.wait_ge(b_widened, B)
            pe.wait_ge(zeroed, 3)
            for c in range(CH):
                pe.wait_ge(v_early, 16 * len(V_PIECES))
                input_product(0, 0, c)
                turn_decay(1, 1, c)
            block_steps(0, True)
            pe.wait_ge(b_widened, 2 * B)
            with nc.tensor.Fori(1, BLOCKS) as k:
                block_steps(k, False)
            for c in range(CH):
                output_product(L - 1, BLOCKS - 1, TB - 1, c)
            for c in range(CH):
                pe.wait_ge(decayed_done[c], L + 2)
                row_scale_product(BLOCKS, c)

        @block.vector
        def _(dve):
            count = [0]

            def chained(ins):
                count[0] += 1
                ins.then_inc(dve_chain, 1)
                dve.wait_ge(dve_chain, count[0])

            def half_of_decay_arguments(T, slot):
                dve.tensor_tensor(ring[:, slot, 1, :, :].rearrange("p c (b n) -> p (c b) n", n=N),
                                  dt_cols[:, 1, bass.ds(T, B, step=L)].unsqueeze(2).broadcast_to([P, B, N]),
                                  a_exp[:, 1, :].unsqueeze(1).broadcast_to([P, B, N]),
                                  ALU.mult).then_inc(z_high, 1)

            dve.memset(tanh_bias[:, :], -DT_C * 0.5 / (DT_R + 1e-8)).then_inc(zeroed, 1)
            for c in range(CH):
                dve.memset(decayed[c][:, :], 0.0).then_inc(decayed_done[c], 1)
                dve.memset(scale[c][:, TB - 1:TB], 1.0).then_inc(decayed_done[c], 1)
            dve.memset(dt_cols[:, :, TOK:TOK + AHEAD], 0.0).then_inc(pad_zeroed, 1)
            for c in range(CH):
                dve.memset(b_wide[c][:, L * P:(L + 1) * P], 0.0).then_inc(zeroed, 1)
            dve.wait_ge(consts_in, 80)
            def negate(j):
                dve.wait_ge(bias_added, j + 1)
                p = dt_rows[:, j * D:(j + 1) * D]
                dve.scalar_tensor_tensor(out=v_work[:, j * D:(j + 1) * D], in0=p, scalar=-1.0, in1=p,
                                         op0=ALU.mult, op1=ALU.min).then_inc(negated, 1)

            for j in range(TILES):
                dve.wait_ge(projected, j + 1)
                dve.tensor_copy(bc[:, j * N:(j + 1) * N], proj_ps[j % 4][:, D:D + N])
                dve.tensor_tensor(dt_rows[:, j * D:(j + 1) * D], proj_ps[j % 4][:, 0:D], bdt[:, :], ALU.add)\
                    .then_inc(bias_added, 1)
                if j:
                    negate(j - 1)
            negate(TILES - 1)
            dve.tensor_copy(b_pc[:, 0, :], bc).then_inc(b_split, 1)
            dve.wait_ge(b_split, 1)
            chained(dve.tensor_tensor(b_work, bc, b_pc[:, 0, :], ALU.subtract))
            dve.tensor_copy(b_pc[:, 1, :], b_work).then_inc(b_split, 1)
            dve.wait_ge(b_split, 2)
            dve.tensor_tensor(b_pc[:, 2, :], b_work, b_pc[:, 1, :], ALU.subtract).then_inc(b_split, 1)

            def copy_c(*which):
                for j in which:
                    dve.wait_ge(c_projected, j + 1)
                    dve.tensor_copy(c_rows[:, j * (TOK // 4):(j + 1) * (TOK // 4)],
                                    (y_ps + norm_ps)[j][0:N, 0:TOK // 4]).then_inc(c_copied, 1)

            for i in range(2):
                dve.wait_ge(softplus_ln, i + 1)
                dve.scalar_tensor_tensor(out=half(dt_rows, i), in0=half(dt_rows, i), scalar=0.0, in1=half(v_work, i),
                                         op0=ALU.max, op1=ALU.add).then_inc(dt_done, 1)
                copy_c(2 * i)
            for i in range(2):
                dve.wait_ge(dt_tanh, i + 1)
                dve.tensor_scalar(half(dt_rows, i), half(dt_rows, i), 2.0 * DT_R, DT_C, ALU.mult, ALU.add)\
                    .then_inc(dt_scaled, 1)
                dve.wait_ge(dt_scaled, i + 1)
                dve.wait_ge(x_rows_in, 16)
                dve.tensor_tensor(half(v_work, i), half(dt_rows, i), half(x_rows, i), ALU.mult).then_inc(v_made, 1)
            copy_c(1, 3)
            for i in range(2):
                dve.wait_ge(v_hi_done, i + 1)
                dve.tensor_tensor(half(v_work, i), half(v_work, i), half(v_hi, i), ALU.subtract).then_inc(v_rest_done, 1)
            for i in range(2):
                dve.wait_ge(v_mid_done, i + 1)
                dve.tensor_tensor(half(v_lo, i), half(v_work, i), half(v_mid, i), ALU.subtract).then_inc(v_lo_done, 1)
            dve.wait_ge(dt_cols_done, TILES)
            dve.wait_ge(a_ready, 2)
            dve.wait_ge(v_lo_done, 2)
            for T in range(AHEAD):
                half_of_decay_arguments(T, T)
            dve.wait_ge(b_loaded, 16 * len(V_PIECES))
            for b in range(B - ACT_WIDENS):
                wide, b_all, own = widening(b, 0)
                dve.tensor_scalar(wide, b_all, own, None, ALU.mult).then_inc(b_widened, 1)

            def state(T, s, c):
                if isinstance(T, int) and T == 0:
                    dve.wait_ge(input_done[c], 1)
                    dve.wait_ge(decayed_done[c], 2)
                dve.wait_ge(scale_done[c], T + 1)
                dve.scalar_tensor_tensor(out=h[c][s % 2], in0=decayed[c][:, :], scalar=scale[c][:, (s - 1) % TB:(s - 1) % TB + 1],
                                         in1=input_ps[c][:, 0:D],
                                         op0=ALU.mult, op1=ALU.add).then_inc(h_done[c], 1)

            def decay(T, s, c):
                dve.wait_ge(h_done[c], T + 1)
                dve.wait_ge(decay_turned[c], AHEAD + T + 2)
                dve.tensor_tensor(decayed[c][:, :], h[c][s % 2], decay_ps[c][:, 0:D], ALU.mult)\
                    .then_inc(decayed_done[c], 1)

            def clamp_norm(T, c):
                dve.wait_ge(normsq_done[c], T + 1)
                dve.tensor_scalar(clamped[c][:, :], norm_ps[c][:, 0:1], 1.0, 2e-8 / CLAMP, ALU.max, ALU.add)\
                    .then_inc(clamped_done[c], 1)

            def take_row_scale(k, c):
                dve.wait_ge(rowscale_done[c], k)
                dve.tensor_copy(row_scale[c][:, :], decay_ps[c][:, D:D + 1]).then_inc(rowscale_copied[c], 1)

            def residual(k, c):
                dve.wait_ge(rowscale_copied[c], k)
                dve.wait_ge(y_taken[c], k + 1)
                dve.wait_ge(xskip_done[c], k + 1)
                dve.scalar_tensor_tensor(out=res[c], in0=y_rows[c][:, :], scalar=row_scale[c][:, :], in1=x_skip[c],
                                         op0=ALU.mult, op1=ALU.add).then_inc(x_skip_free[c], 1)

            def statistics(k, c):
                dve.wait_ge(x_skip_free[c], k + 1)
                dve.bn_stats(stats[c][:, :], res[c]).then_inc(stats_done[c], 1)

            def aggregate(c):
                dve.bn_aggr(moments[c][:, :], stats[c][:, :]).then_inc(moments_done[c], 1)

            def variance(k, c):
                dve.wait_ge(moments_done[c], k)
                dve.tensor_scalar(var_eps[c][:, :], moments[c][:, 1:2], EPS, None, ALU.add).then_inc(var_done[c], 1)

            def normalise(k, c):
                dve.wait_ge(rstd_done[c], k)
                dve.wait_ge(x1_stored[c], 16 * k)
                dve.tensor_scalar(normed[c], res[c], moments[c][:, 0:1], rstd[c][:, :],
                                  ALU.subtract, ALU.mult).then_inc(normed_done[c], 1)

            def block_steps(k, first):
                for s in range(TB):
                    T = k * TB + s
                    if s in (6, 7) and not first:
                        dve.wait_ge(stats_done[s - 6], k)
                    state(T, s, 0)
                    if s or not first:
                        clamp_norm(T - 1, 1)
                    half_of_decay_arguments(T + AHEAD, (s + AHEAD) % TB)
                    if s == 2 and not first:
                        take_row_scale(k, 0)
                    decay(T, s, 0)
                    state(T, s, 1)
                    clamp_norm(T, 0)
                    if s == 2 and not first:
                        take_row_scale(k, 1)
                    decay(T, s, 1)
                    if first:
                        wide, b_all, own = widening(s, 1)
                        dve.tensor_scalar(wide, b_all, own, None, ALU.mult).then_inc(b_widened, 1)
                    if not first:
                        if s in (2, 3):
                            residual(k, s - 2)
                        if s in (4, 5):
                            statistics(k, s - 4)
                        if s in (6, 7):
                            aggregate(s - 6)
                        if s in (8, 9):
                            variance(k, s - 8)
                        if s in (12, 13):
                            normalise(k, s - 12)

            block_steps(0, True)
            with nc.vector.Fori(1, BLOCKS) as k:
                block_steps(k, False)
            clamp_norm(L - 1, 1)
            for c in range(CH):
                take_row_scale(BLOCKS, c)
            for c in range(CH):
                residual(BLOCKS, c)
            for c in range(CH):
                statistics(BLOCKS, c)
            for c in range(CH):
                dve.wait_ge(stats_done[c], BLOCKS)
                aggregate(c)
            for c in range(CH):
                variance(BLOCKS, c)
            for c in range(CH):
                normalise(BLOCKS, c)


S = 375
SK = 3
SC = S // SK
F = 1024
FC = F // P
PAIRS = B // 2
GATES = 3
GROUP = 4
SCORE = 1.0 / 16.0


def decoder_and_cell(nc, used, a, x1, out):
    with ExitStack() as ctx:
        def sb(name, shape, dt=F32):
            return ctx.enter_context(nc.sbuf_tensor(name, shape, dt))

        def sb2(name, shape, dt=F32):
            return [sb(f"{name}{j}", shape, dt) for j in range(2)]

        def pb(name):
            return ctx.enter_context(nc.psum_tensor(name, [P, 512], F32))

        def sem(name):
            used.append(nc.alloc_semaphore(name))
            return used[-1]

        def sem2(name):
            return [sem(f"{name}{j}") for j in range(2)]

        const = sb("const_b", [P, a["consts"].shape[1]])
        ident = const[:, 0:P]
        ident_l = const[0:L, 0:L]
        causal = const[0:L, 2 * P + CB + B:2 * P + CB + B + L]
        w1 = sb("w1", [P, DH, F])
        w2 = sb("w2", [P, FC, D])
        gate_w = sb("gate_w", [P, DH, 2, 4, D])
        vectors = sb("vectors", [P, FC + GATES * DH + DH])
        b1 = vectors[:, 0:FC]
        gate_b = vectors[:, FC:FC + GATES * DH].rearrange("p (g h) -> p g h", g=GATES)
        in_c = vectors[:, FC + GATES * DH:FC + GATES * DH + DH]
        norm_w = sb("norm_w", [L, 8, D])
        minus_half = sb("minus_half_b", [P, GROUP])
        ones_l = sb("ones_l", [P, L])
        spare = sb("spare", [P, 1])
        x1_att = sb2("x1_att", [L, D])
        x1_res = sb2("x1_res", [L, D])
        x1_cols = sb2("x1_cols", [P, DH, L])
        self_s = sb2("self_s", [L, L])
        self_p = sb2("self_p", [L, L])
        self_pt = sb2("self_pt", [L, L])
        ctx_cols = sb2("ctx_cols", [P, DH, S])
        ctx_rows = sb2("ctx_rows", [SC, SK, D])
        cross_p = sb2("cross_p", [L, S])
        cross_pt = sb2("cross_pt", [SC, SK, L])
        neg_max = [sb2(f"neg_max{i}", [L, 1]) for i in range(2)]
        row_max = [sb2(f"row_max{i}", [L, 1]) for i in range(2)]
        row_sum = [sb2(f"row_sum{i}", [L, 1]) for i in range(2)]
        inv_sum = [sb2(f"inv_sum{i}", [L, 1]) for i in range(2)]
        ln_in = [sb2(f"ln_in{i}", [L, D]) for i in range(4)]
        ln_out = [sb2(f"ln_out{i}", [L, D]) for i in range(2)]
        ln_stats = [sb2(f"ln_stats{i}", [L, 6]) for i in range(4)]
        ln_mv = [sb2(f"ln_mv{i}", [L, 2]) for i in range(4)]
        ln_var = [sb2(f"ln_var{i}", [L, 1]) for i in range(4)]
        ln_rstd = [sb2(f"ln_rstd{i}", [L, 1]) for i in range(4)]
        y1_cols = sb2("y1_cols", [P, DH, L])
        y2_bias = sb2("y2_bias", [L, D])
        y2_cols = sb("y2_cols", [P, DH, 2, L])
        hidden = sb("hidden", [P, FC, 2, L])
        x2_cols = sb2("x2_cols", [P, DH, L])
        fresh = sb2("fresh", [L, 2, D])
        all_rows = sb("all_rows", [L, 2, B, D])
        x2_all, wo_all = all_rows[:, 0, :, :], all_rows[:, 1, :, :]
        gate_t = sb("gate_t", [P, GATES, DH, L])
        cell2 = sb("cell2", [P, DH, L])
        kept = sb("kept", [P, DH, L])
        added = sb("added", [P, DH, L])
        base = sb("base", [L, D])
        fin_stats = sb("fin_stats", [L, B, 6])
        fin_mv = sb("fin_mv", [L, B, 2])
        fin_var = sb("fin_var", [L, B])
        fin_rstd = sb("fin_rstd", [L, B])
        fin_bias = sb("fin_bias", [L, B])

        att_ps = [pb(f"att_ps{j}") for j in range(2)]
        ff1_ps = [pb(f"ff1_ps{i}") for i in range(2)]
        ff2_ps = [pb(f"ff2_ps{j}") for j in range(2)]
        gate_ps = [pb(f"gate_ps{i}") for i in range(2)]

        small_in = sem("small_in")
        w_in = sem("w_in")
        n_in = sem("n_in")
        setup = sem("setup")
        gate_b_halved = sem("gate_b_halved")
        u_halved = sem("u_halved")
        ones_done = sem("ones_done")
        x1_in, x1r_in, ctx_in = sem2("x1_in"), sem2("x1r_in"), sem2("ctx_in")
        x1_turned, x1_cols_done = sem2("x1_turned"), sem2("x1_cols_done")
        self_scored, self_masked, self_max, self_neg, self_exp = (
            sem2("self_scored"), sem2("self_masked"), sem2("self_max"), sem2("self_neg"), sem2("self_exp"))
        self_inv, self_turned, self_pt_done, self_mixed = (
            sem2("self_inv"), sem2("self_turned"), sem2("self_pt_done"), sem2("self_mixed"))
        y1_turned, y1_cols_done = sem2("y1_turned"), sem2("y1_cols_done")
        cross_scored, cross_max, cross_neg, cross_exp = (
            sem2("cross_scored"), sem2("cross_max"), sem2("cross_neg"), sem2("cross_exp"))
        cross_inv, cross_turned, cross_pt_done, cross_mixed = (
            sem2("cross_inv"), sem2("cross_turned"), sem2("cross_pt_done"), sem2("cross_mixed"))
        y2_turned, y2_cols_done, y2_bias_done = sem2("y2_turned"), sem2("y2_cols_done"), sem2("y2_bias_done")
        ff1_done, hidden_done = sem("ff1_done"), sem("hidden_done")
        ff2_done = sem2("ff2_done")
        ln_summed = [sem2(f"ln_summed{i}") for i in range(4)]
        ln_stat = [sem2(f"ln_stat{i}") for i in range(4)]
        ln_agg = [sem2(f"ln_agg{i}") for i in range(4)]
        ln_vared = [sem2(f"ln_vared{i}") for i in range(4)]
        ln_rooted = [sem2(f"ln_rooted{i}") for i in range(4)]
        ln_centred = [sem2(f"ln_centred{i}") for i in range(3)]
        ln_done = [sem2(f"ln_done{i}") for i in (0, 1)]
        x2_done = sem2("x2_done")
        x1_beta_done = sem2("x1_beta_done")
        x2_turned, x2_cols_done, rows_kept = sem2("x2_turned"), sem2("x2_cols_done"), sem2("rows_kept")
        wo_done, wo_copied = sem2("wo_done"), sem2("wo_copied")
        gates_done, gates_tanh = sem("gates_done"), sem("gates_tanh")
        cell_kept, cell_added, cell_done = sem("cell_kept"), sem("cell_added"), sem("cell_done")
        u_done, base_done = sem("u_done"), sem("base_done")
        fin_arg, fin_tanh, fin_sum, fin_stat, fin_agg, fin_vared, fin_rooted, fin_normed = (
            sem("fin_arg"), sem("fin_tanh"), sem("fin_sum"), sem("fin_stat"), sem("fin_agg"), sem("fin_vared"),
            sem("fin_rooted"), sem("fin_normed"))
        fin_arg_last, fin_offset, fin_normed_last = sem("fin_arg_last"), sem("fin_offset"), sem("fin_normed_last")
        fin_sum_later = sem("fin_sum_later")
        out_stored = sem("out_stored")

        def add_base(eng, q):
            t = wo_all[:, q * GROUP:(q + 1) * GROUP, :]
            return eng.tensor_tensor(t, t, base[:, :].unsqueeze(1).broadcast_to([L, GROUP, D]), ALU.add)

        def add_tanh(eng, q):
            x = x2_all[:, q * GROUP:(q + 1) * GROUP, :]
            return eng.tensor_tensor(x, x, wo_all[:, q * GROUP:(q + 1) * GROUP, :], ALU.add)

        block = ctx.enter_context(nc.Block())

        @block.sync
        def _(sp):
            def pair_of(dram, p, j):
                return dram.rearrange("(p j) r c -> p j r c", j=2)[bass.ds(p, 1), j]

            def kept_rows(q, j):
                return all_rows[:, :, :, :].rearrange("t w (p j) d -> t w p j d", j=2)[:, :, bass.ds(q, 1), j, :]\
                    .rearrange("t w b d -> t w (b d)")

            def load_rows(p, first=False):
                for j in range(2):
                    if not first:
                        sp.wait_ge(self_mixed[j], p)
                        sp.wait_ge(ln_summed[0][j], p)
                    sp.dma_start(x1_att[j][:, :], pair_of(x1, p, j).rearrange("b t d -> (b t) d"))\
                        .then_inc(x1_in[j], 16)

            def load_context(p, first=False):
                for j in range(2):
                    if not first:
                        sp.wait_ge(cross_mixed[j], p)
                    sp.dma_start(ctx_cols[j][:, :, :],
                                 pair_of(a["ctxT"], p, j).rearrange("b (h p) s -> p (b h) s", p=P))\
                        .then_inc(ctx_in[j], 16)
                    sp.dma_start(ctx_rows[j][:, :, :],
                                 pair_of(a["ctx_1024"], p, j).rearrange("b (k s) d -> s (b k) d", s=SC))\
                        .then_inc(ctx_in[j], 16)

            def load_residual(q, first=False):
                for j in range(2):
                    if not first:
                        sp.wait_ge(ln_summed[3][j], q)
                    sp.dma_start(x1_res[j][:, :], pair_of(x1, q, j).rearrange("b t d -> (b t) d"))\
                        .then_inc(x1r_in[j], 16)

            def keep(q):
                for j in range(2):
                    sp.wait_ge(wo_copied[j], q + 2)
                    sp.dma_start(kept_rows(q, j), fresh[j][:, :, :]).then_inc(rows_kept[j], 16)

            sp.dma_start(const[:, :], a["consts"]).then_inc(small_in, 16)
            load_rows(0, True)
            sp.dma_start(vectors[:, :], a["vectors"]).then_inc(small_in, 16)
            sp.dma_start(norm_w[:, :, :], a["row_vectors"].unsqueeze(0).broadcast_to([L, 8, D])).then_inc(n_in, 16)
            load_context(0, True)
            load_residual(0, True)
            sp.dma_start(w1[:, :, :], a["L0_xattn_w1"].rearrange("(h p) f -> p h f", p=P)).then_inc(w_in, 16)
            sp.dma_start(w2[:, :, :], a["L0_xattn_w2"].rearrange("(c p) d -> p c d", p=P)).then_inc(w_in, 16)
            sp.dma_start(gate_w[:, :, :, :, :], a["gateT"].rearrange("(h p) (w g n) -> p h w g n", p=P, w=2, g=4))\
                .then_inc(w_in, 16)
            load_rows(1)
            load_context(1)
            with nc.sync.Fori(1, PAIRS - 1) as p:
                load_rows(p + 1)
                load_residual(p)
                load_context(p + 1)
                keep(p - 1)
            load_residual(PAIRS - 1)
            keep(PAIRS - 2)
            keep(PAIRS - 1)
            for g in range(B // GROUP):
                if g < B // GROUP - 1:
                    sp.wait_ge(fin_normed, GROUP * (g + 1))
                else:
                    sp.wait_ge(fin_normed_last, GROUP)
                sp.dma_start(out[g * GROUP:(g + 1) * GROUP].rearrange("b t d -> t b d"),
                             x2_all[:, g * GROUP:(g + 1) * GROUP, :]).then_inc(out_stored, 16)
            sp.wait_ge(out_stored, 16 * (B // GROUP))

        @block.gpsimd
        def _(g):
            def root(i, p, j):
                g.wait_ge(ln_vared[i][j], p + 1)
                g.tensor_tensor(ln_rstd[i][j][:, :], ln_var[i][j][:, :], minus_half[0:L, 0:1], ALU.pow)\
                    .then_inc(ln_rooted[i][j], 1)

            def add_b2(p, j):
                g.wait_ge(ln_done[1][j], p + 1)
                g.tensor_tensor(y2_bias[j][:, :], ln_out[1][j][:, :], norm_w[:, 6, :], ALU.add)\
                    .then_inc(y2_bias_done[j], 1)

            def add_beta3(q, j):
                g.wait_ge(x1r_in[j], 16 * (q + 1))
                g.tensor_tensor(x1_res[j][:, :], x1_res[j][:, :], norm_w[:, 5, :], ALU.add)\
                    .then_inc(x1_beta_done[j], 1)

            def pair_step(p, q):
                if q is not None:
                    add_beta3(q, 0)
                    add_beta3(q, 1)
                if p is not None:
                    root(0, p, 0)
                    root(0, p, 1)
                if q is not None:
                    for j in range(2):
                        root(2, q, j)
                        root(3, q, j)
                if p is not None:
                    for j in range(2):
                        root(1, p, j)
                    for j in range(2):
                        add_b2(p, j)

            g.memset(minus_half[:, :], -0.5).then_inc(setup, 1)
            g.wait_ge(setup, 1)
            g.wait_ge(n_in, 16)
            pair_step(0, None)
            with nc.gpsimd.Fori(1, PAIRS) as p:
                pair_step(p, p - 1)
            pair_step(None, PAIRS - 1)
            g.wait_ge(base_done, 1)
            for j in range(2):
                g.wait_ge(rows_kept[j], 16 * (PAIRS + 1))
            add_base(g, B // GROUP - 1).then_inc(fin_arg_last, 1)

            def final_root(q):
                g.wait_ge(fin_vared, q + 1)
                g.tensor_tensor(fin_rstd[:, q * GROUP:(q + 1) * GROUP], fin_var[:, q * GROUP:(q + 1) * GROUP],
                                minus_half[0:L, :], ALU.pow).then_inc(fin_rooted, 1)

            half = B // GROUP // 2
            for q in range(half):
                g.wait_ge(fin_tanh, half + q + 1)
                add_tanh(g, half + q).then_inc(fin_sum_later, 1)
                final_root(q)
            for q in range(half, B // GROUP):
                final_root(q)

        @block.scalar
        def _(act):
            def copy(dst, src, done):
                act.activation(dst, src, ACT.Copy).then_inc(done, 1)

            def columns(ps):
                return ps[:, 0:DH * L].rearrange("p (h t) -> p h t", h=DH)

            def relu(q, u):
                act.wait_ge(ff1_done, q * (FC // 2) + u + 1)
                for i in range(2):
                    c = 2 * u + i
                    act.activation(hidden[:, c, :, :].rearrange("p j t -> p (j t)"),
                                   ff1_ps[u % 2][:, i * 2 * L:(i + 1) * 2 * L], ACT.Relu, bias=b1[:, c:c + 1])\
                        .then_inc(hidden_done, 1)

            def gate_tanh(q, j):
                act.wait_ge(gates_done, 2 * q + j + 1)
                for g in range(GATES):
                    for hf in range(DH):
                        ps = gate_ps[g // 2][:, ((g % 2) * DH + hf) * L:((g % 2) * DH + hf + 1) * L]
                        act.activation(gate_t[:, g, hf, :], ps, ACT.Tanh, bias=gate_b[:, g, hf:hf + 1],
                                       scale=0.5 if g < 2 else 1.0).then_inc(gates_tanh, 1)

            def copy_x2(q, j):
                act.wait_ge(x2_turned[j], q + 1)
                copy(x2_cols[j][:, :, :], columns(ff2_ps[j]), x2_cols_done[j])

            def copy_wo(q, j):
                act.wait_ge(wo_done[j], q + 1)
                act.wait_ge(rows_kept[j], 16 * (q + 1))
                copy(fresh[j][:, 1, :], ff2_ps[j][0:L, 0:D], wo_copied[j])

            def columns_of(turned, cols, done, p):
                for j in range(2):
                    act.wait_ge(turned[j], p + 1)
                    copy(cols[j], columns(att_ps[j]), done[j])

            def cross_exponent(p, j):
                act.wait_ge(cross_neg[j], p + 1)
                act.activation(cross_p[j][:, :], att_ps[j][0:L, 0:S], ACT.Exp, bias=neg_max[1][j][:, :],
                               scale=SCORE, accum_out=row_sum[1][j][:, :]).then_inc(cross_exp[j], 1)

            def pair_step(p, q):
                if p is not None:
                    columns_of(x1_turned, [t[:, :, :] for t in x1_cols], x1_cols_done, p)
                if q is not None:
                    relu(q, 0)
                    relu(q, 1)
                if p is not None:
                    for j in range(2):
                        act.wait_ge(self_neg[j], p + 1)
                        act.activation(self_p[j][:, :], self_s[j][:, :], ACT.Exp, bias=neg_max[0][j][:, :],
                                       accum_out=row_sum[0][j][:, :]).then_inc(self_exp[j], 1)
                if q is not None:
                    relu(q, 2)
                if p is not None:
                    for j in range(2):
                        act.wait_ge(self_turned[j], p + 1)
                        copy(self_pt[j][:, :], att_ps[j][0:L, 0:L], self_pt_done[j])
                if q is not None:
                    relu(q, 3)
                if p is not None:
                    columns_of(y1_turned, [t[:, :, :] for t in y1_cols], y1_cols_done, p)
                if q is not None:
                    copy_x2(q, 0)
                if p is not None:
                    cross_exponent(p, 0)
                    cross_exponent(p, 1)
                if q is not None:
                    gate_tanh(q, 0)
                if p is not None:
                    for j in range(2):
                        act.wait_ge(cross_turned[j], p + 1)
                        copy(cross_pt[j][:, :, :], att_ps[j][0:SC, 0:SK * L].rearrange("p (k t) -> p k t", k=SK),
                             cross_pt_done[j])
                if q is not None:
                    copy_wo(q, 0)
                    copy_x2(q, 1)
                if p is not None:
                    columns_of(y2_turned, [y2_cols[:, :, j, :] for j in range(2)], y2_cols_done, p)
                if q is not None:
                    gate_tanh(q, 1)
                    copy_wo(q, 1)

            for j in range(2):
                act.sem_inc(wo_copied[j], 1)
            act.wait_ge(small_in, 32)
            act.wait_ge(gate_b_halved, 1)
            pair_step(0, None)
            with nc.scalar.Fori(1, PAIRS) as p:
                pair_step(p, p - 1)
            pair_step(None, PAIRS - 1)
            for q in range(B // GROUP):
                if q < B // GROUP - 1:
                    act.wait_ge(fin_arg, q + 1)
                else:
                    act.wait_ge(fin_arg_last, 1)
                t = wo_all[:, q * GROUP:(q + 1) * GROUP, :]
                act.activation(t, t, ACT.Tanh).then_inc(fin_tanh, 1)
            for q in range(B // GROUP - 1):
                act.wait_ge(fin_offset, q + 1)
                for b in range(q * GROUP, (q + 1) * GROUP):
                    act.activation(x2_all[:, b, :], x2_all[:, b, :], ACT.Identity, bias=fin_bias[:, b:b + 1],
                                   scale=fin_rstd[:, b:b + 1]).then_inc(fin_normed, 1)

        @block.tensor
        def _(pe):
            def turn(ps, rows, width, done, src, identity):
                for i in range(width // P):
                    mm = pe.transpose(ps[:, i * L:i * L + L], src[:, i * P:(i + 1) * P], identity)
                mm.then_inc(done, 1)

            def self_turn_x1(p, j):
                pe.wait_ge(x1_in[j], 16 * (p + 1))
                if not isinstance(p, int):
                    pe.wait_ge(y2_cols_done[j], p)
                turn(att_ps[j], L, D, x1_turned[j], x1_att[j], ident_l)

            def self_scores(p, j):
                pe.wait_ge(x1_cols_done[j], p + 1)
                for hf in range(DH):
                    mm = pe.matmul(att_ps[j][0:L, 0:L], x1_cols[j][:, hf, :], x1_cols[j][:, hf, :],
                                   start=(hf == 0), stop=(hf == DH - 1))
                mm.then_inc(self_scored[j], 1)

            def self_turn(p, j):
                pe.wait_ge(self_exp[j], p + 1)
                pe.transpose(att_ps[j][0:L, 0:L], self_p[j][:, :], ident_l).then_inc(self_turned[j], 1)

            def self_mix(p, j):
                pe.wait_ge(self_pt_done[j], p + 1)
                pe.matmul(att_ps[j][0:L, 0:D], self_pt[j][:, :], x1_att[j][:, :], start=True, stop=True)\
                    .then_inc(self_mixed[j], 1)

            def turn_y1(p, j):
                pe.wait_ge(ln_done[0][j], p + 1)
                turn(att_ps[j], L, D, y1_turned[j], ln_out[0][j], ident_l)

            def cross_scores(p, j):
                pe.wait_ge(y1_cols_done[j], p + 1)
                pe.wait_ge(ctx_in[j], 32 * (p + 1))
                for hf in range(DH):
                    mm = pe.matmul(att_ps[j][0:L, 0:S], y1_cols[j][:, hf, :], ctx_cols[j][:, hf, :],
                                   start=(hf == 0), stop=(hf == DH - 1))
                mm.then_inc(cross_scored[j], 1)

            def cross_turn(p, j):
                pe.wait_ge(cross_exp[j], p + 1)
                for k in range(SK):
                    mm = pe.transpose(att_ps[j][0:SC, k * L:(k + 1) * L], cross_p[j][:, k * SC:(k + 1) * SC], ident_l)
                mm.then_inc(cross_turned[j], 1)

            def cross_mix(p, j):
                pe.wait_ge(cross_pt_done[j], p + 1)
                for k in range(SK):
                    mm = pe.matmul(att_ps[j][0:L, 0:D], cross_pt[j][:, k, :], ctx_rows[j][:, k, :],
                                   start=(k == 0), stop=(k == SK - 1))
                mm.then_inc(cross_mixed[j], 1)

            def turn_y2(p, j):
                pe.wait_ge(ln_done[1][j], p + 1)
                turn(att_ps[j], L, D, y2_turned[j], ln_out[1][j], ident_l)

            def feed_forward_1(q, u):
                if u == 0:
                    for j in range(2):
                        pe.wait_ge(y2_cols_done[j], q + 1)
                if u >= 2:
                    pe.wait_ge(hidden_done, q * FC + 2 * (u - 1))
                for i in range(2):
                    c = 2 * u + i
                    for hf in range(DH):
                        mm = pe.matmul(ff1_ps[u % 2][:, i * 2 * L:(i + 1) * 2 * L], w1[:, hf, c * P:(c + 1) * P],
                                       y2_cols[:, hf, :, :].rearrange("p j t -> p (j t)"),
                                       start=(hf == 0), stop=(hf == DH - 1))
                mm.then_inc(ff1_done, 1)

            def feed_forward_2(q, j, chunks):
                if chunks.start == 0:
                    pe.wait_ge(hidden_done, (q + 1) * FC)
                    pe.wait_ge(wo_copied[j], q + 1)
                for c in chunks:
                    mm = pe.matmul(ff2_ps[j][0:L, 0:D], hidden[:, c, j, :], w2[:, c, :],
                                   start=(c == 0), stop=(c == FC - 1))
                if chunks.stop == FC:
                    mm.then_inc(ff2_done[j], 1)

            def turn_x2(q, j):
                pe.wait_ge(x2_done[j], q + 1)
                turn(ff2_ps[j], L, D, x2_turned[j], fresh[j][:, 0, :], ident_l)

            def gates(q, j):
                pe.wait_ge(x2_cols_done[j], q + 1)
                pe.wait_ge(cell_done, 2 * q + j + 1)
                for g in range(GATES):
                    for m in range(DH):
                        o = gate_ps[g // 2][:, ((g % 2) * DH + m) * L:((g % 2) * DH + m + 1) * L]
                        for w, cols in enumerate((x2_cols[j], cell2)):
                            for hf in range(DH):
                                mm = pe.matmul(o, gate_w[:, hf, w, g, m * P:(m + 1) * P], cols[:, hf, :],
                                               start=(w == 0 and hf == 0), stop=(w == 1 and hf == DH - 1))
                mm.then_inc(gates_done, 1)

            def output_x(q, j):
                for hf in range(DH):
                    mm = pe.matmul(ff2_ps[j][0:L, 0:D], x2_cols[j][:, hf, :], gate_w[:, hf, 0, 3, :],
                                   start=(hf == 0), stop=(hf == DH - 1))
                mm.then_inc(wo_done[j], 1)

            def pair_step(p, q):
                def both(stage):
                    if p is not None:
                        for j in range(2):
                            stage(p, j)

                def feed(stage, *which):
                    if q is not None:
                        stage(q, *which)

                both(self_turn_x1)
                feed(feed_forward_1, 0)
                feed(feed_forward_1, 1)
                both(self_scores)
                feed(feed_forward_1, 2)
                both(self_turn)
                feed(feed_forward_1, 3)
                both(self_mix)
                feed(feed_forward_2, 0, range(FC))
                feed(feed_forward_2, 1, range(FC // 2))
                both(turn_y1)
                feed(feed_forward_2, 1, range(FC // 2, FC))
                if p is not None:
                    cross_scores(p, 0)
                feed(turn_x2, 0)
                if p is not None:
                    cross_scores(p, 1)
                feed(gates, 0)
                both(cross_turn)
                feed(output_x, 0)
                feed(turn_x2, 1)
                both(cross_mix)
                feed(gates, 1)
                both(turn_y2)
                feed(output_x, 1)

            pe.wait_ge(small_in, 32)
            pair_step(0, None)
            pe.wait_ge(w_in, 48)
            pe.wait_ge(u_halved, 2)
            with nc.tensor.Fori(1, PAIRS) as p:
                pair_step(p, p - 1)
            pair_step(None, PAIRS - 1)
            pe.wait_ge(cell_done, B + 1)
            pe.wait_ge(wo_copied[0], PAIRS + 1)
            for hf in range(DH):
                mm = pe.matmul(ff2_ps[0][0:L, 0:D], cell2[:, hf, :], gate_w[:, hf, 1, 3, :],
                               start=(hf == 0), stop=(hf == DH - 1))
            mm.then_inc(u_done, 1)

        @block.vector
        def _(dve):
            def self_softmax(p, j):
                dve.wait_ge(self_scored[j], p + 1)
                dve.scalar_tensor_tensor(out=self_s[j][:, :], in0=att_ps[j][0:L, 0:L], scalar=SCORE, in1=causal,
                                         op0=ALU.mult, op1=ALU.add).then_inc(self_masked[j], 1)
                dve.wait_ge(self_masked[j], p + 1)
                dve.reduce_max(row_max[0][j][:, :], self_s[j][:, :], mybir.AxisListType.X).then_inc(self_max[j], 1)
                dve.wait_ge(self_max[j], p + 1)
                dve.tensor_scalar(neg_max[0][j][:, :], row_max[0][j][:, :], -1.0, None, ALU.mult)\
                    .then_inc(self_neg[j], 1)

            def self_inverse(p, j):
                dve.wait_ge(self_exp[j], p + 1)
                dve.reciprocal(inv_sum[0][j][:, :], row_sum[0][j][:, :]).then_inc(self_inv[j], 1)

            def cross_largest(p, j):
                dve.wait_ge(cross_scored[j], p + 1)
                dve.reduce_max(row_max[1][j][:, :], att_ps[j][0:L, 0:S], mybir.AxisListType.X).then_inc(cross_max[j], 1)
                dve.wait_ge(cross_max[j], p + 1)
                dve.tensor_scalar(neg_max[1][j][:, :], row_max[1][j][:, :], -SCORE, None, ALU.mult)\
                    .then_inc(cross_neg[j], 1)

            def cross_inverse(p, j):
                dve.wait_ge(cross_exp[j], p + 1)
                dve.reciprocal(inv_sum[1][j][:, :], row_sum[1][j][:, :]).then_inc(cross_inv[j], 1)

            def attention_residual(i, p, j):
                dve.wait_ge((self_mixed, cross_mixed)[i][j], p + 1)
                dve.wait_ge((self_inv, cross_inv)[i][j], p + 1)
                if i == 0:
                    dve.wait_ge(x1_in[j], 16 * (p + 1))
                else:
                    dve.wait_ge(ln_done[0][j], p + 1)
                dve.scalar_tensor_tensor(out=ln_in[i][j][:, :], in0=att_ps[j][0:L, 0:D], scalar=inv_sum[i][j][:, :],
                                         in1=(x1_att[j], ln_out[0][j])[i][:, :], op0=ALU.mult, op1=ALU.add)\
                    .then_inc(ln_summed[i][j], 1)

            def feed_residual(q, j):
                dve.wait_ge(ff2_done[j], q + 1)
                dve.wait_ge(y2_bias_done[j], q + 1)
                dve.tensor_tensor(ln_in[2][j][:, :], ff2_ps[j][0:L, 0:D], y2_bias[j][:, :], ALU.add)\
                    .then_inc(ln_summed[2][j], 1)

            def statistics(i, p, js):
                for j in js:
                    dve.wait_ge(ln_summed[i][j], p + 1)
                    dve.bn_stats(ln_stats[i][j][:, :], ln_in[i][j][:, :]).then_inc(ln_stat[i][j], 1)
                for j in js:
                    dve.wait_ge(ln_stat[i][j], p + 1)
                dve.memset(spare[:, :], 0.0)
                for j in js:
                    dve.bn_aggr(ln_mv[i][j][:, :], ln_stats[i][j][:, :]).then_inc(ln_agg[i][j], 1)
                for j in js:
                    dve.wait_ge(ln_agg[i][j], p + 1)
                    dve.tensor_scalar(ln_var[i][j][:, :], ln_mv[i][j][:, 1:2], EPS, None, ALU.add)\
                        .then_inc(ln_vared[i][j], 1)
                if i < 3:
                    for j in js:
                        centre(i, p, j)

            def centre(i, p, j):
                dve.scalar_tensor_tensor(out=ln_in[i][j][:, :], in0=ln_in[i][j][:, :], scalar=ln_mv[i][j][:, 0:1],
                                         in1=norm_w[:, 2 * i, :], op0=ALU.subtract, op1=ALU.mult)\
                    .then_inc(ln_centred[i][j], 1)

            def normalise(i, p, j):
                dve.wait_ge(ln_centred[i][j], p + 1)
                dve.wait_ge(ln_rooted[i][j], p + 1)
                dve.scalar_tensor_tensor(out=ln_out[i][j][:, :], in0=ln_in[i][j][:, :], scalar=ln_rstd[i][j][:, :],
                                         in1=norm_w[:, 2 * i + 1, :], op0=ALU.mult, op1=ALU.add)\
                    .then_inc(ln_done[i][j], 1)

            def outer_residual(q, j):
                dve.wait_ge(ln_centred[2][j], q + 1)
                dve.wait_ge(ln_rooted[2][j], q + 1)
                dve.wait_ge(x1_beta_done[j], q + 1)
                dve.scalar_tensor_tensor(out=ln_in[3][j][:, :], in0=ln_in[2][j][:, :], scalar=ln_rstd[2][j][:, :],
                                         in1=x1_res[j][:, :], op0=ALU.mult, op1=ALU.add)\
                    .then_inc(ln_summed[3][j], 1)

            def normalise_x2(q, j):
                dve.wait_ge(ln_rooted[3][j], q + 1)
                dve.wait_ge(rows_kept[j], 16 * (q + 1))
                dve.tensor_scalar(fresh[j][:, 0, :], ln_in[3][j][:, :], ln_mv[3][j][:, 0:1], ln_rstd[3][j][:, :],
                                  ALU.subtract, ALU.mult).then_inc(x2_done[j], 1)

            def cell(q, j):
                n = 2 * q + j + 1
                dve.wait_ge(gates_tanh, GATES * DH * n)
                dve.scalar_tensor_tensor(out=kept[:, :, :], in0=gate_t[:, 0, :, :], scalar=1.0, in1=cell2[:, :, :],
                                         op0=ALU.add, op1=ALU.mult).then_inc(cell_kept, 1)
                dve.scalar_tensor_tensor(out=added[:, :, :], in0=gate_t[:, 1, :, :], scalar=1.0, in1=gate_t[:, 2, :, :],
                                         op0=ALU.add, op1=ALU.mult).then_inc(cell_added, 1)
                dve.wait_ge(cell_kept, n)
                dve.wait_ge(cell_added, n)
                dve.scalar_tensor_tensor(out=cell2[:, :, :], in0=kept[:, :, :], scalar=0.5, in1=added[:, :, :],
                                         op0=ALU.mult, op1=ALU.add).then_inc(cell_done, 1)

            def pair_step(p, q):
                if p is not None:
                    for j in range(2):
                        self_softmax(p, j)
                    for j in range(2):
                        self_inverse(p, j)
                    for j in range(2):
                        attention_residual(0, p, j)
                    statistics(0, p, (0, 1))
                    for j in range(2):
                        normalise(0, p, j)
                if q is not None:
                    feed_residual(q, 0)
                    statistics(2, q, (0,))
                    outer_residual(q, 0)
                    statistics(3, q, (0,))
                    feed_residual(q, 1)
                    normalise_x2(q, 0)
                    statistics(2, q, (1,))
                if p is not None:
                    for j in range(2):
                        cross_largest(p, j)
                if q is not None:
                    outer_residual(q, 1)
                    statistics(3, q, (1,))
                    normalise_x2(q, 1)
                if p is not None:
                    for j in range(2):
                        cross_inverse(p, j)
                if q is not None:
                    cell(q, 0)
                if p is not None:
                    for j in range(2):
                        attention_residual(1, p, j)
                    statistics(1, p, (0, 1))
                    for j in range(2):
                        normalise(1, p, j)
                if q is not None:
                    cell(q, 1)

            for j in range(2):
                dve.sem_inc(rows_kept[j], 16)
            dve.memset(ones_l[:, :], 1.0).then_inc(ones_done, 1)
            dve.wait_ge(small_in, 32)
            dve.tensor_scalar(gate_b[:, 0:2, :], gate_b[:, 0:2, :], 0.5, None, ALU.mult).then_inc(gate_b_halved, 1)
            dve.wait_ge(ones_done, 1)
            for hf in range(DH):
                ins = dve.tensor_scalar(cell2[:, hf, :], ones_l[:, :], in_c[:, hf:hf + 1], 2.0, ALU.mult, ALU.mult)
            ins.then_inc(cell_done, 1)
            dve.wait_ge(n_in, 16)
            pair_step(0, None)
            dve.wait_ge(w_in, 48)
            for hf in range(DH):
                u = gate_w[:, hf, 1, :, :]
                dve.tensor_scalar(u, u, 0.5, None, ALU.mult).then_inc(u_halved, 1)
            with nc.vector.Fori(1, PAIRS) as p:
                pair_step(p, p - 1)
            pair_step(None, PAIRS - 1)
            dve.wait_ge(u_done, 1)
            dve.wait_ge(n_in, 16)
            dve.tensor_tensor(base[:, :], ff2_ps[0][0:L, 0:D], norm_w[:, 7, :], ALU.add).then_inc(base_done, 1)
            dve.wait_ge(base_done, 1)
            for j in range(2):
                dve.wait_ge(rows_kept[j], 16 * (PAIRS + 1))
            for q in range(B // GROUP - 1):
                add_base(dve, q).then_inc(fin_arg, 1)

            def offset(q):
                dve.wait_ge(fin_rooted, q + 1)
                r = slice(q * GROUP, (q + 1) * GROUP)
                dve.scalar_tensor_tensor(out=fin_bias[:, r], in0=fin_mv[:, r, 0], scalar=-1.0, in1=fin_rstd[:, r],
                                         op0=ALU.mult, op1=ALU.mult).then_inc(fin_offset, 1)

            def finish(q):
                r = range(q * GROUP, (q + 1) * GROUP)
                half = B // GROUP // 2
                if q < half:
                    dve.wait_ge(fin_tanh, q + 1)
                    add_tanh(dve, q).then_inc(fin_sum, 1)
                    dve.wait_ge(fin_sum, q + 1)
                else:
                    dve.wait_ge(fin_sum_later, q - half + 1)
                for b in r:
                    dve.bn_stats(fin_stats[:, b, :], x2_all[:, b, :]).then_inc(fin_stat, 1)
                if q:
                    offset(q - 1)
                dve.wait_ge(fin_stat, r.stop)
                for b in r:
                    dve.bn_aggr(fin_mv[:, b, :], fin_stats[:, b, :]).then_inc(fin_agg, 1)
                dve.wait_ge(fin_agg, r.stop)
                dve.tensor_scalar(fin_var[:, r.start:r.stop], fin_mv[:, r.start:r.stop, 1], EPS, None, ALU.add)\
                    .then_inc(fin_vared, 1)

            for q in range(B // GROUP):
                finish(q)
            dve.wait_ge(fin_rooted, B // GROUP)
            for b in range(B - GROUP, B):
                dve.tensor_scalar(x2_all[:, b, :], x2_all[:, b, :], fin_mv[:, b, 0:1], fin_rstd[:, b:b + 1],
                                  ALU.subtract, ALU.mult).then_inc(fin_normed_last, 1)


_DIRECT = ['x', 'ctx_1024', 'L0_attn_bdt', 'L0_attn_A_log', 'L0_attn_Dp', 'L0_xattn_w1', 'L0_xattn_w2']
_ROW_VECTORS = ['L0_xattn_g1', 'L0_xattn_beta1', 'L0_xattn_g2', 'L0_xattn_beta2', 'L0_xattn_g3', 'L0_xattn_beta3',
                'L0_xattn_b2', 'L0_ffn_bo']


def build(nc, args, out):
    x1 = nc.dram_tensor("x1", (B, L, D), F32, kind="Internal").ap()
    used = []
    state_space(nc, used, args, x1)
    nc.clear_and_free_semaphores(used)
    nc.all_engine_barrier()
    decoder_and_cell(nc, [], args, x1, out)


def kernel(**inputs):
    import numpy as _np
    import concourse.bacc as _bacc
    from concourse import mybir as _mybir
    from concourse.bass_utils import run_bass_kernel_spmd as _run

    def turned(names):
        return _np.ascontiguousarray(_np.concatenate([_np.asarray(inputs[n]).T for n in names], axis=1))

    nc = _bacc.Bacc("TRN2", target_bir_lowering=False, num_devices=1)
    laid = {name: _np.ascontiguousarray(inputs[name]) for name in _DIRECT}
    laid["xT"] = _np.ascontiguousarray(_np.asarray(inputs["x"]).reshape(TOK, D).T)
    laid["ctxT"] = _np.ascontiguousarray(_np.asarray(inputs["ctx_1024"]).transpose(0, 2, 1))
    laid["projT"] = turned(["L0_attn_Wdt", "L0_attn_WB", "L0_attn_WC"])
    laid["gateT"] = turned([f"L0_ffn_{w}{g}" for w in "wu" for g in "fico"])
    laid["vectors"] = _np.ascontiguousarray(_np.concatenate(
        [_np.asarray(inputs[n]).reshape(-1, P) for n in
         ("L0_xattn_b1", "L0_ffn_bf", "L0_ffn_bi", "L0_ffn_bc", "L0_ffn_in_c")], axis=0).T)
    laid["row_vectors"] = _np.stack([_np.asarray(inputs[n]) for n in _ROW_VECTORS])
    laid["consts"] = shape_constants()
    args = {n: nc.dram_tensor(f"in_{n}", a.shape, _mybir.dt.from_np(a.dtype), kind="ExternalInput").ap()
            for n, a in laid.items()}
    out = nc.dram_tensor("out_0", (B, L, D), F32, kind="ExternalOutput").ap()
    build(nc, args, out)
    r = _run(nc, [{f"in_{n}": a for n, a in laid.items()}], core_ids=[0])
    return r.results[0]["out_0"]
```
